# Optimizing a Trainium2 kernel written in Bass

```python
import numpy as np
import jax
import jax.numpy as jnp

def _softmax(x, axis=-1):
    return jax.nn.softmax(x, axis=axis)

def _gelu(x):
    return jax.nn.gelu(x, approximate=True)

def _silu(x):
    return jax.nn.silu(x)

def _sigmoid(x):
    return jax.nn.sigmoid(x)

def _layernorm(x, axis=-1, eps=1e-05):
    m = jnp.mean(x, axis=axis, keepdims=True)
    v = jnp.var(x, axis=axis, keepdims=True)
    return (x - m) / jnp.sqrt(v + eps)

def _scatter_add(tgt, idx, src, axis=0):
    return tgt.at[idx].add(src)

def _segment_sum(src, seg, n):
    return jax.ops.segment_sum(src, seg, n)
kernel_name = 'mk_dlrm_tower_d1_rec_r8_c8d416'

def setup_inputs(seed: int=0):
    np.random.seed(seed)
    _w = jnp.asarray

    def _rec_inputs():
        import jax
        import jax.numpy as jnp
        _tk = jax.random.key(seed)
        dense_ctx = jax.random.normal(jax.random.fold_in(_tk, 190), (512, 16), jnp.float32)
        ids = jnp.stack([jax.random.randint(jax.random.fold_in(_tk, 200 + f), (512,), 0, v, jnp.int32) for f, v in enumerate([1000, 1250, 125000, 1250, 1000, 1250, 1250, 125000, 1250, 125000, 125000, 125000, 12500, 1000, 125000, 125000, 12500, 1000, 1250, 125000, 1250, 125000, 12500, 1250, 12500, 125000, 1000, 1000, 1250, 1000, 1250, 12500, 1000, 1250, 1000, 125000, 1000, 1000, 125000])], axis=1)
        tbl_0 = 0.05 * jax.random.normal(jax.random.fold_in(_tk, 500 + 0), (1000, 16), jnp.float32)
        tbl_1 = 0.05 * jax.random.normal(jax.random.fold_in(_tk, 500 + 1), (1250, 16), jnp.float32)
        tbl_2 = 0.05 * jax.random.normal(jax.random.fold_in(_tk, 500 + 2), (125000, 16), jnp.float32)
        tbl_3 = 0.05 * jax.random.normal(jax.random.fold_in(_tk, 500 + 3), (1250, 16), jnp.float32)
        tbl_4 = 0.05 * jax.random.normal(jax.random.fold_in(_tk, 500 + 4), (1000, 16), jnp.float32)
        tbl_5 = 0.05 * jax.random.normal(jax.random.fold_in(_tk, 500 + 5), (1250, 16), jnp.float32)
        tbl_6 = 0.05 * jax.random.normal(jax.random.fold_in(_tk, 500 + 6), (1250, 16), jnp.float32)
        tbl_7 = 0.05 * jax.random.normal(jax.random.fold_in(_tk, 500 + 7), (125000, 16), jnp.float32)
        tbl_8 = 0.05 * jax.random.normal(jax.random.fold_in(_tk, 500 + 8), (1250, 16), jnp.float32)
        tbl_9 = 0.05 * jax.random.normal(jax.random.fold_in(_tk, 500 + 9), (125000, 16), jnp.float32)
        tbl_10 = 0.05 * jax.random.normal(jax.random.fold_in(_tk, 500 + 10), (125000, 16), jnp.float32)
        tbl_11 = 0.05 * jax.random.normal(jax.random.fold_in(_tk, 500 + 11), (125000, 16), jnp.float32)
        tbl_12 = 0.05 * jax.random.normal(jax.random.fold_in(_tk, 500 + 12), (12500, 16), jnp.float32)
        tbl_13 = 0.05 * jax.random.normal(jax.random.fold_in(_tk, 500 + 13), (1000, 16), jnp.float32)
        tbl_14 = 0.05 * jax.random.normal(jax.random.fold_in(_tk, 500 + 14), (125000, 16), jnp.float32)
        tbl_15 = 0.05 * jax.random.normal(jax.random.fold_in(_tk, 500 + 15), (125000, 16), jnp.float32)
        tbl_16 = 0.05 * jax.random.normal(jax.random.fold_in(_tk, 500 + 16), (12500, 16), jnp.float32)
        tbl_17 = 0.05 * jax.random.normal(jax.random.fold_in(_tk, 500 + 17), (1000, 16), jnp.float32)
        tbl_18 = 0.05 * jax.random.normal(jax.random.fold_in(_tk, 500 + 18), (1250, 16), jnp.float32)
        tbl_19 = 0.05 * jax.random.normal(jax.random.fold_in(_tk, 500 + 19), (125000, 16), jnp.float32)
        tbl_20 = 0.05 * jax.random.normal(jax.random.fold_in(_tk, 500 + 20), (1250, 16), jnp.float32)
        tbl_21 = 0.05 * jax.random.normal(jax.random.fold_in(_tk, 500 + 21), (125000, 16), jnp.float32)
        tbl_22 = 0.05 * jax.random.normal(jax.random.fold_in(_tk, 500 + 22), (12500, 16), jnp.float32)
        tbl_23 = 0.05 * jax.random.normal(jax.random.fold_in(_tk, 500 + 23), (1250, 16), jnp.float32)
        tbl_24 = 0.05 * jax.random.normal(jax.random.fold_in(_tk, 500 + 24), (12500, 16), jnp.float32)
        tbl_25 = 0.05 * jax.random.normal(jax.random.fold_in(_tk, 500 + 25), (125000, 16), jnp.float32)
        tbl_26 = 0.05 * jax.random.normal(jax.random.fold_in(_tk, 500 + 26), (1000, 16), jnp.float32)
        tbl_27 = 0.05 * jax.random.normal(jax.random.fold_in(_tk, 500 + 27), (1000, 16), jnp.float32)
        tbl_28 = 0.05 * jax.random.normal(jax.random.fold_in(_tk, 500 + 28), (1250, 16), jnp.float32)
        tbl_29 = 0.05 * jax.random.normal(jax.random.fold_in(_tk, 500 + 29), (1000, 16), jnp.float32)
        tbl_30 = 0.05 * jax.random.normal(jax.random.fold_in(_tk, 500 + 30), (1250, 16), jnp.float32)
        tbl_31 = 0.05 * jax.random.normal(jax.random.fold_in(_tk, 500 + 31), (12500, 16), jnp.float32)
        tbl_32 = 0.05 * jax.random.normal(jax.random.fold_in(_tk, 500 + 32), (1000, 16), jnp.float32)
        tbl_33 = 0.05 * jax.random.normal(jax.random.fold_in(_tk, 500 + 33), (1250, 16), jnp.float32)
        tbl_34 = 0.05 * jax.random.normal(jax.random.fold_in(_tk, 500 + 34), (1000, 16), jnp.float32)
        tbl_35 = 0.05 * jax.random.normal(jax.random.fold_in(_tk, 500 + 35), (125000, 16), jnp.float32)
        tbl_36 = 0.05 * jax.random.normal(jax.random.fold_in(_tk, 500 + 36), (1000, 16), jnp.float32)
        tbl_37 = 0.05 * jax.random.normal(jax.random.fold_in(_tk, 500 + 37), (1000, 16), jnp.float32)
        tbl_38 = 0.05 * jax.random.normal(jax.random.fold_in(_tk, 500 + 38), (125000, 16), jnp.float32)
        _rk = jax.random.fold_in(_tk, 7)
        W_top1 = 0.05 * jax.random.normal(jax.random.fold_in(_tk, 801), (400, 512), jnp.float32)
        W_top2 = 0.0441942 * jax.random.normal(jax.random.fold_in(_tk, 802), (512, 256), jnp.float32)
        W_top3 = 0.0625 * jax.random.normal(jax.random.fold_in(_tk, 803), (256, 1), jnp.float32)
        b_top1 = jnp.zeros((512,), jnp.float32)
        b_top2 = jnp.zeros((256,), jnp.float32)
        return (dense_ctx, ids, tbl_0, tbl_1, tbl_2, tbl_3, tbl_4, tbl_5, tbl_6, tbl_7, tbl_8, tbl_9, tbl_10, tbl_11, tbl_12, tbl_13, tbl_14, tbl_15, tbl_16, tbl_17, tbl_18, tbl_19, tbl_20, tbl_21, tbl_22, tbl_23, tbl_24, tbl_25, tbl_26, tbl_27, tbl_28, tbl_29, tbl_30, tbl_31, tbl_32, tbl_33, tbl_34, tbl_35, tbl_36, tbl_37, tbl_38, W_top1, b_top1, W_top2, b_top2, W_top3)
    dense_ctx, ids, tbl_0, tbl_1, tbl_2, tbl_3, tbl_4, tbl_5, tbl_6, tbl_7, tbl_8, tbl_9, tbl_10, tbl_11, tbl_12, tbl_13, tbl_14, tbl_15, tbl_16, tbl_17, tbl_18, tbl_19, tbl_20, tbl_21, tbl_22, tbl_23, tbl_24, tbl_25, tbl_26, tbl_27, tbl_28, tbl_29, tbl_30, tbl_31, tbl_32, tbl_33, tbl_34, tbl_35, tbl_36, tbl_37, tbl_38, W_top1, b_top1, W_top2, b_top2, W_top3 = _rec_inputs()

    def _L0_rec_setup():
        import jax, jax.numpy as jnp
        import numpy as np
        B, F0, D = (512, 39, 16)
        CIN = [128, 128, 128]

        def _cin_layer(X0, Xi, W, b):
            H = W.shape[0]
            F0_, Fi = (X0.shape[1], Xi.shape[1])
            Wr = W.reshape(H, F0_, Fi)
            return jnp.einsum('hjk,bjd,bkd->bhd', Wr, X0, Xi) + b[None, :, None]
        key = jax.random.key(seed)
        ks = jax.random.split(key, 4)
        x = jax.random.normal(ks[0], (B, F0, D), dtype=jnp.float32)
        fields = [F0] + CIN
        inp = {'embedded_features': x}
        for i in range(len(CIN)):
            cin = F0 * fields[i]
            cout = fields[i + 1]
            kw = jax.random.fold_in(ks[1], i)
            inp[f'W{i}'] = jax.random.normal(kw, (cout, cin), dtype=jnp.float32) / np.sqrt(cin)
            inp[f'b{i}'] = jnp.zeros((cout,), dtype=jnp.float32)
        return inp
    _L0_rec_all = _L0_rec_setup()
    _L0_rec_in = {k: v for k, v in _L0_rec_all.items() if k in ('W0', 'b0', 'W1', 'b1', 'W2', 'b2')}
    del _L0_rec_all
    return {'dense_ctx': dense_ctx, 'ids': ids, 'tbl_0': tbl_0, 'tbl_1': tbl_1, 'tbl_2': tbl_2, 'tbl_3': tbl_3, 'tbl_4': tbl_4, 'tbl_5': tbl_5, 'tbl_6': tbl_6, 'tbl_7': tbl_7, 'tbl_8': tbl_8, 'tbl_9': tbl_9, 'tbl_10': tbl_10, 'tbl_11': tbl_11, 'tbl_12': tbl_12, 'tbl_13': tbl_13, 'tbl_14': tbl_14, 'tbl_15': tbl_15, 'tbl_16': tbl_16, 'tbl_17': tbl_17, 'tbl_18': tbl_18, 'tbl_19': tbl_19, 'tbl_20': tbl_20, 'tbl_21': tbl_21, 'tbl_22': tbl_22, 'tbl_23': tbl_23, 'tbl_24': tbl_24, 'tbl_25': tbl_25, 'tbl_26': tbl_26, 'tbl_27': tbl_27, 'tbl_28': tbl_28, 'tbl_29': tbl_29, 'tbl_30': tbl_30, 'tbl_31': tbl_31, 'tbl_32': tbl_32, 'tbl_33': tbl_33, 'tbl_34': tbl_34, 'tbl_35': tbl_35, 'tbl_36': tbl_36, 'tbl_37': tbl_37, 'tbl_38': tbl_38, 'W_top1': W_top1, 'b_top1': b_top1, 'W_top2': W_top2, 'b_top2': b_top2, 'W_top3': W_top3, 'L0_rec_W0': _L0_rec_in['W0'], 'L0_rec_b0': _L0_rec_in['b0'], 'L0_rec_W1': _L0_rec_in['W1'], 'L0_rec_b1': _L0_rec_in['b1'], 'L0_rec_W2': _L0_rec_in['W2'], 'L0_rec_b2': _L0_rec_in['b2']}

def reference(dense_ctx, ids, tbl_0, tbl_1, tbl_2, tbl_3, tbl_4, tbl_5, tbl_6, tbl_7, tbl_8, tbl_9, tbl_10, tbl_11, tbl_12, tbl_13, tbl_14, tbl_15, tbl_16, tbl_17, tbl_18, tbl_19, tbl_20, tbl_21, tbl_22, tbl_23, tbl_24, tbl_25, tbl_26, tbl_27, tbl_28, tbl_29, tbl_30, tbl_31, tbl_32, tbl_33, tbl_34, tbl_35, tbl_36, tbl_37, tbl_38, W_top1, b_top1, W_top2, b_top2, W_top3, L0_rec_W0, L0_rec_b0, L0_rec_W1, L0_rec_b1, L0_rec_W2, L0_rec_b2):
    import jax
    import jax.numpy as jnp

    def _L0_rec_ref(embedded_features, W0, b0, W1, b1, W2, b2):
        import jax, jax.numpy as jnp
        import numpy as np
        B, F0, D = (512, 39, 16)
        CIN = [128, 128, 128]

        def _cin_layer(X0, Xi, W, b):
            H = W.shape[0]
            F0_, Fi = (X0.shape[1], Xi.shape[1])
            Wr = W.reshape(H, F0_, Fi)
            return jnp.einsum('hjk,bjd,bkd->bhd', Wr, X0, Xi) + b[None, :, None]
        X0 = embedded_features
        Ws = [(W0, b0), (W1, b1), (W2, b2)]
        Xi = X0
        res = []
        for W, b in Ws:
            Xi = _cin_layer(X0, Xi, W, b)
            res.append(Xi.sum(axis=2))
        return jnp.concatenate(res, axis=1)
    e = jnp.stack([tbl_0[ids[:, 0]], tbl_1[ids[:, 1]], tbl_2[ids[:, 2]], tbl_3[ids[:, 3]], tbl_4[ids[:, 4]], tbl_5[ids[:, 5]], tbl_6[ids[:, 6]], tbl_7[ids[:, 7]], tbl_8[ids[:, 8]], tbl_9[ids[:, 9]], tbl_10[ids[:, 10]], tbl_11[ids[:, 11]], tbl_12[ids[:, 12]], tbl_13[ids[:, 13]], tbl_14[ids[:, 14]], tbl_15[ids[:, 15]], tbl_16[ids[:, 16]], tbl_17[ids[:, 17]], tbl_18[ids[:, 18]], tbl_19[ids[:, 19]], tbl_20[ids[:, 20]], tbl_21[ids[:, 21]], tbl_22[ids[:, 22]], tbl_23[ids[:, 23]], tbl_24[ids[:, 24]], tbl_25[ids[:, 25]], tbl_26[ids[:, 26]], tbl_27[ids[:, 27]], tbl_28[ids[:, 28]], tbl_29[ids[:, 29]], tbl_30[ids[:, 30]], tbl_31[ids[:, 31]], tbl_32[ids[:, 32]], tbl_33[ids[:, 33]], tbl_34[ids[:, 34]], tbl_35[ids[:, 35]], tbl_36[ids[:, 36]], tbl_37[ids[:, 37]], tbl_38[ids[:, 38]]], axis=1)
    z = _L0_rec_ref(e, L0_rec_W0, L0_rec_b0, L0_rec_W1, L0_rec_b1, L0_rec_W2, L0_rec_b2)
    z = z.reshape(z.shape[0], -1)
    h = jnp.concatenate([z, dense_ctx], axis=1)
    h = jnp.maximum(h @ W_top1 + b_top1, 0.0)
    h = jnp.maximum(h @ W_top2 + b_top2, 0.0)
    y = h @ W_top3
    return y

_drawn_inputs = setup_inputs


def setup_inputs(seed=0):
    import zlib

    import numpy as np

    out = dict(_drawn_inputs(seed))
    spreads = {'b_top1': (0.0, 0.1),
     'b_top2': (0.0, 0.1),
     'L0_rec_b0': (0.0, 0.1),
     'L0_rec_b1': (0.0, 0.1),
     'L0_rec_b2': (0.0, 0.1)}
    factors = {'tbl_0': 8.0,
     'tbl_1': 5.827,
     'tbl_2': 5.312,
     'tbl_3': 7.027,
     'tbl_4': 8.0,
     'tbl_5': 8.0,
     'tbl_6': 8.0,
     'tbl_7': 6.841,
     'tbl_8': 8.0,
     'tbl_9': 8.0,
     'tbl_10': 8.0,
     'tbl_11': 6.657,
     'tbl_12': 8.0,
     'tbl_13': 8.0,
     'tbl_14': 4.509,
     'tbl_15': 5.831,
     'tbl_16': 8.0,
     'tbl_17': 8.0,
     'tbl_18': 8.0,
     'tbl_19': 5.936,
     'tbl_20': 7.137,
     'tbl_21': 8.0,
     'tbl_22': 8.0,
     'tbl_23': 8.0,
     'tbl_24': 8.0,
     'tbl_25': 7.452,
     'tbl_26': 5.842,
     'tbl_27': 8.0,
     'tbl_28': 8.0,
     'tbl_29': 8.0,
     'tbl_30': 6.984,
     'tbl_31': 6.623,
     'tbl_32': 8.0,
     'tbl_33': 6.797,
     'tbl_34': 8.0,
     'tbl_35': 7.382,
     'tbl_36': 8.0,
     'tbl_37': 6.762,
     'tbl_38': 8.0,
     'L0_rec_W0': 3.32}
    for name, (base, spread) in spreads.items():
        noise = np.random.default_rng([zlib.crc32(name.encode()), seed]).standard_normal(out[name].shape)
        drawn = base * np.exp(spread * noise) if base else spread * noise
        out[name] = jnp.asarray(drawn.astype(out[name].dtype))
    for name, factor in factors.items():
        out[name] = (out[name] * factor).astype(out[name].dtype)
    return out
```

```python
from contextlib import ExitStack

import concourse.bass as bass
from concourse import mybir

ALU = mybir.AluOpType
ACT = mybir.ActivationFunctionType
AX_X = mybir.AxisListType.X
F32 = mybir.dt.float32
F32R = mybir.dt.float32r
I32 = mybir.dt.int32

P = 128
B = 512
F = 39
D = 16
H = 128
TB = P // D
BLOCKS = B // P
TILES = P // TB
QT = 4
QUADS = TILES // QT
QN = QT * P
SHIFTS = (F + 1) // 2
SPC = 3
CHUNKS = -(-SHIFTS // SPC)
REP = SPC * F
SETS = 4
PER_SET = D // SETS

SIZES = [4] * 9 + [3]
FIRST = [sum(SIZES[:g]) for g in range(len(SIZES))]
GROUPS = len(SIZES)
YBANKS = 5
KIND = "ADAADADAAD"
DVE_GROUPS = [g for g in range(GROUPS) if KIND[g] == "D"]
ACT_GROUPS = [g for g in range(GROUPS) if KIND[g] == "A"]
POOLED = 4
DVE_STEPS = sum(SIZES[g] for g in DVE_GROUPS)
DVE_DONE = {g: sum(SIZES[x] for x in DVE_GROUPS if x <= g) for g in DVE_GROUPS}
ACT_STEPS = len(ACT_GROUPS)
POOL_STEPS = POOLED - 1
JOIN_STEPS = ACT_STEPS - POOLED + 4
GATHERS = [list(range(F))[4 * t:4 * t + 4] for t in range(TILES)]

PREP_W1 = GROUPS
PREP_W2 = GROUPS
PREP_W0 = 2
PREP = PREP_W1 + PREP_W2 + PREP_W0 + 1


def chunk_rows(c):
    return F * min(SPC, SHIFTS - SPC * c)


def build(nc, dense_ctx, ids, tables, W_top1, b_top1, W_top2, b_top2, W_top3, W0, b0, W1, b1, W2, b2, out):
    K1 = W_top1.shape[0]
    M1 = W_top1.shape[1]
    M2 = W_top2.shape[1]
    C = dense_ctx.shape[1]
    MC1, MC2 = M1 // P, M2 // P
    w2t_dram = nc.dram_tensor("w2t_dram", (P, F * H), F32, kind="Internal").ap()
    dense_t_dram = nc.dram_tensor("dense_t_dram", (C, B), F32, kind="Internal").ap()

    with ExitStack() as ctx:
        def sb(name, shape, dt=F32):
            return ctx.enter_context(nc.sbuf_tensor(name, shape, dt))

        def sem(name):
            return ctx.enter_context(nc.semaphore(name))

        ps_y = ctx.enter_context(nc.psum_tensor("ps_y", [P, YBANKS, 512], F32))
        ps_x1 = ctx.enter_context(nc.psum_tensor("ps_x1", [P, 512], F32))
        ps_tr = ctx.enter_context(nc.psum_tensor("ps_tr", [P, 512], F32))
        ps_g = ctx.enter_context(nc.psum_tensor("ps_g", [P, 512], F32))

        w1_hi = sb("w1_hi", [P, F * H], F32R)
        w1_lo = sb("w1_lo", [P, F * H], F32R)
        w0t = sb("w0t", [P, CHUNKS, H])
        g_all = sb("g_all", [P, F + 1, B])
        x0 = sb("x0", [P, TILES * P])
        bz = sb("bz", [P, 2, CHUNKS, QN])
        emb = sb("emb", [P, SPC, F, D])
        ids_cur = sb("ids_cur", [P, F], I32)
        ident = sb("ident", [P, P])
        mask = sb("mask", [P, TB])
        x1_hi = sb("x1_hi", [P, 2, QN], F32R)
        x1_lo = sb("x1_lo", [P, 2, QN], F32R)
        xt = sb("xt", [P, 2, QT, F])
        bd = sb("bd", [P, 2, QT, F + 1, TB])
        prod = sb("prod", [P, ACT_STEPS, 4 * H])
        part = sb("part", [P, 2, 4 * H])
        acc = sb("acc", [P, 2, 2, H])
        x2 = sb("x2", [P, 2, H])
        r1 = sb("r1", [P, B])
        r3 = w0t[:].rearrange("p c h -> p (c h)")[:, 0:B]
        dense_sb = sb("dense_sb", [P, BLOCKS, C])
        b1_row = sb("b1_row", [P, H])
        b0_col = sb("b0_col", [P, 1])
        b2_col = sb("b2_col", [P, 1])
        b02_sum = sb("b02_sum", [P, 2])
        bt1 = sb("bt1", [P, MC1])
        bt2 = sb("bt2", [P, MC2])
        wt3 = sb("wt3", [P, MC2])
        y_row = part[:, 0, :]

        flat_g = g_all[:].rearrange("p j b -> p (j b)")
        w1_in = flat_g[:, 0:F * H]
        w2_in = flat_g[:, F * H:2 * F * H]
        w2_out = flat_g[:, 2 * F * H:3 * F * H]
        dense_out = flat_g[0:C, 3 * F * H:3 * F * H + B]
        w0_in = flat_g[:, 3 * F * H + B:3 * F * H + B + F * F]
        w0_sym = bz[:].rearrange("p a c n -> p (a c n)")[:, CHUNKS * QN:CHUNKS * QN + SHIFTS * F]
        late = bz[:].rearrange("p a c n -> p (a c n)")
        w2t = late[:, 0:F * H]
        dense_t = late[0:C, F * H:F * H + B]
        wt2 = late[:, F * H + B:F * H + B + MC1 * M2].rearrange("p (c m) -> p c m", c=MC1)
        wt1 = x0[:].rearrange("p (c m) -> p c m", m=M1)
        h1 = g_all
        h2 = g_all[:, MC1:MC1 + MC2, :]

        ids_ld = sem("ids_ld")
        w0_ld, w1_ld, w2_ld, small_ld = sem("w0_ld"), sem("w1_ld"), sem("w2_ld"), sem("small_ld")
        ident_zero, ident_made = sem("ident_zero"), sem("ident_made")
        mask_made = sem("mask_made")
        w0_summed = sem("w0_summed")
        bsum_made = sem("bsum_made")
        ones_made = sem("ones_made")
        prep_tr, prep_act, prep_dve = sem("prep_tr"), sem("prep_act"), sem("prep_dve")
        w2_saved = sem("w2_saved")
        gathered = sem("gathered")
        emb_made = sem("emb_made")
        emb_turned, x0_made = sem("emb_turned"), sem("x0_made")
        shifted = [sem("shifted_0"), sem("shifted_1")]
        z_made, x1_summed = sem("z_made"), sem("x1_summed")
        x1_hi_made, x1_lo_made = sem("x1_hi_made"), sem("x1_lo_made")
        xt_turned, xt_made, bd_made = sem("xt_turned"), sem("xt_made"), sem("bd_made")
        y_made = sem("y_made")
        dve_step, act_step, pool_step = sem("dve_step"), sem("act_step"), sem("pool_step")
        join_step = sem("join_step")
        g_summed, g_kept = sem("g_summed"), sem("g_kept")
        late_w2, late_mlp = sem("late_w2"), sem("late_mlp")
        r1_done, r3_summed, r3_made = sem("r1_done"), sem("r3_summed"), sem("r3_made")
        h1_summed, h1_made = sem("h1_summed"), sem("h1_made")
        h2_summed, h2_made = sem("h2_summed"), sem("h2_made")
        y_summed, y_out, stored = sem("y_summed"), sem("y_out"), sem("stored")

        block = ctx.enter_context(nc.Block())

        @block.sync
        def _(sp):
            def shift_fields(qi):
                for s in range(SHIFTS):
                    lo = (s % SPC) * F
                    sp.dma_start(bz[lo:lo + F, qi % 2, s // SPC, :],
                                 x0[s:s + F, qi * QN:(qi + 1) * QN]).then_inc(shifted[qi % 2], 16)

            sp.dma_start(ids_cur[:], ids[0:P, :]).then_inc(ids_ld, 16)
            sp.dma_start(w0_in, W0).then_inc(w0_ld, 16)
            sp.dma_start(w1_in, W1).then_inc(w1_ld, 16)
            sp.dma_start(w2_in, W2).then_inc(w2_ld, 16)
            sp.dma_start(dense_sb[:], dense_ctx.rearrange("(c p) d -> p c d", p=P)).then_inc(small_ld, 16)
            sp.dma_start(b1_row[:], b1.rearrange("(a h) -> a h", a=1).broadcast_to([P, H])).then_inc(small_ld, 16)
            for dst, src in ((b0_col[:], b0), (b2_col[:], b2), (bt1[:], b_top1), (bt2[:], b_top2)):
                sp.dma_start(dst, src.rearrange("(c p) -> p c", p=P),
                             allow_slow_non_contiguous=True).then_inc(small_ld, 16)
            sp.dma_start(wt3[:], W_top3.rearrange("(c p) a -> p (c a)", p=P),
                         allow_slow_non_contiguous=True).then_inc(small_ld, 16)

            sp.wait_ge(x0_made, SETS)
            shift_fields(0)
            sp.wait_ge(prep_act, PREP)
            sp.dma_start(w2t_dram, w2_out).then_inc(w2_saved, 16)
            sp.dma_start(dense_t_dram, dense_out).then_inc(w2_saved, 16)

            def block_loads(bt, last):
                if not last:
                    sp.wait_ge(gathered, 16 * F * (bt + 1))
                    sp.dma_start(ids_cur[:], ids[bass.ds((bt + 1) * P, P), :]).then_inc(ids_ld, 16)
                for qi in range(QUADS if not last else QUADS - 1):
                    sp.wait_ge(x1_summed, QUADS * bt + qi + 1)
                    if qi == QUADS - 1:
                        sp.wait_ge(x0_made, SETS * (bt + 2))
                    shift_fields((qi + 1) % QUADS)

            with sp.Fori(0, BLOCKS - 1) as bt:
                block_loads(bt, False)
            block_loads(BLOCKS - 1, True)

            sp.wait_ge(x1_summed, BLOCKS * QUADS + 1)
            sp.wait_ge(w2_saved, 32)
            sp.dma_start(w2t, w2t_dram).then_inc(late_w2, 16)
            sp.dma_start(dense_t, dense_t_dram).then_inc(late_mlp, 16)
            sp.dma_start(wt1[:, 0:K1 // P, :],
                         W_top1[0:K1 // P * P, :].rearrange("(c p) m -> p c m", p=P)).then_inc(late_mlp, 16)
            sp.dma_start(wt1[0:C, K1 // P, :], W_top1[K1 // P * P:K1, :]).then_inc(late_mlp, 16)
            sp.dma_start(wt2, W_top2.rearrange("(c p) m -> p c m", p=P)).then_inc(late_mlp, 16)
            sp.wait_ge(y_out, 1)
            sp.dma_start(out.rearrange("b a -> a b"), y_row[0:1, :]).then_inc(stored, 16)
            sp.wait_ge(stored, 16)

        @block.gpsimd
        def _(pool):
            def gather(f):
                pool.indirect_dma_start(
                    out=emb[:, 0, f, :], out_offset=None, in_=tables[f],
                    in_offset=bass.IndirectOffsetOnAxis(ap=ids_cur[:, f:f + 1], axis=0),
                ).then_inc(gathered, 16)

            nc.gpsimd.memset(ident[:], 0.0).then_inc(ident_zero, 1)
            pool.wait_ge(ident_zero, 1)
            nc.gpsimd.affine_select(out=ident[:], in_=ident[:], compare_op=ALU.not_equal, fill=1.0, base=0,
                                    pattern=[[-1, P]], channel_multiplier=1).then_inc(ident_made, 1)
            pool.wait_ge(ids_ld, 16)
            for f in range(F):
                gather(f)
            pool.sem_inc(pool_step, POOL_STEPS)

            def sum_tile(bt, tau):
                T = TILES * bt + tau
                n = POOL_STEPS * (T + 1)
                a = ACT_STEPS * (T + 1)
                part_t = part[:, tau % 2, :]
                pool.wait_ge(act_step, a + 2)
                pool.wait_ge(join_step, JOIN_STEPS * (T + 1))
                nc.gpsimd.tensor_tensor(part_t, prod[:, 0, :], prod[:, 1, :], ALU.add).then_inc(pool_step, 1)
                for k in range(2, POOLED):
                    pool.wait_ge(act_step, a + k + 1)
                    pool.wait_ge(pool_step, n + k - 1)
                    nc.gpsimd.tensor_tensor(part_t, part_t, prod[:, k, :], ALU.add).then_inc(pool_step, 1)

            def block_sums(bt, last):
                for tau in range(TILES):
                    if not last and tau == 0:
                        pool.wait_ge(ids_ld, 16 * (bt + 2))
                        pool.wait_ge(emb_turned, SETS * (bt + 1))
                    sum_tile(bt, tau)
                    if not last:
                        for f in GATHERS[tau]:
                            gather(f)

            with pool.Fori(0, BLOCKS - 1) as bt:
                block_sums(bt, False)
            block_sums(BLOCKS - 1, True)

        @block.scalar
        def _(act):
            def keep_x0(bt, s):
                act.wait_ge(emb_turned, SETS * bt + s + 1)
                dst = x0[0:REP].rearrange("p (t d b) -> p d t b", d=D, b=TB)[:, PER_SET * s:PER_SET * (s + 1)]
                src = ps_tr[0:REP].rearrange("p (d t b) -> p d t b", d=PER_SET, b=TB)
                nc.scalar.copy(dst, src).then_inc(x0_made, 1)

            def keep_xt(q, par):
                act.wait_ge(xt_turned, q + 1)
                src = ps_tr[:, 0:QT * (F + 1)].rearrange("p (t j) -> p t j", t=QT)[:, :, 0:F]
                nc.scalar.copy(xt[:, par], src).then_inc(xt_made, 1)

            def keep_x1(q, par):
                act.wait_ge(x1_summed, q + 2)
                nc.scalar.activation(x1_hi[:, par, :], ps_x1[:], ACT.Identity,
                                     bias=b0_col[:, 0:1]).then_inc(x1_hi_made, 1)

            for n in range(PREP):
                act.wait_ge(prep_tr, n + 1)
                bank = ps_y[:, n % YBANKS, :]
                if n < PREP_W1 + PREP_W2:
                    g = n % GROUPS
                    cols = slice(FIRST[g] * H, (FIRST[g] + SIZES[g]) * H)
                    dst, src = (w1_hi if n < PREP_W1 else w2_out)[:, cols], bank[:, 0:SIZES[g] * H]
                elif n < PREP - 1:
                    c = 4 * (n - PREP_W1 - PREP_W2)
                    full = [x for x in range(c, min(c + 4, CHUNKS)) if chunk_rows(x) == REP]
                    dst, src = w0t[0:REP, c:c + len(full), :], bank[0:REP, 0:len(full) * H]
                    if c + 4 >= CHUNKS:
                        r = chunk_rows(CHUNKS - 1)
                        nc.scalar.copy(w0t[0:r, CHUNKS - 1, :], bank[0:r, len(full) * H:(len(full) + 1) * H])
                    src = src.rearrange("p (c h) -> p c h", h=H)
                else:
                    dst, src = dense_out, bank[0:C, :]
                nc.scalar.copy(dst, src).then_inc(prep_act, 1)
            act.wait_ge(small_ld, 16 * 7)
            nc.scalar.mul(b02_sum[:, 0:1], b0_col[:], float(D))
            nc.scalar.mul(b02_sum[:, 1:2], b2_col[:], float(D)).then_inc(bsum_made, 1)

            for s in range(SETS):
                keep_x0(0, s)
            keep_xt(0, 0)
            keep_x1(0, 0)
            act.wait_ge(w2_saved, 32)
            act.sem_inc(act_step, ACT_STEPS)
            act.sem_inc(g_kept, 1)

            def scale_groups(bt, qi, ti):
                T = TILES * bt + QT * qi + ti
                for k, g in enumerate(ACT_GROUPS):
                    act.wait_ge(y_made, GROUPS * T + g + 2)
                    if k < POOLED:
                        act.wait_ge(pool_step, POOL_STEPS * T + max(k, 1))
                    else:
                        act.wait_ge(join_step, JOIN_STEPS * (T + 1) + k - POOLED + 1)
                    for m in range(SIZES[g]):
                        ins = nc.scalar.activation(prod[:, k, m * H:(m + 1) * H],
                                                   ps_y[:, g % YBANKS, m * H:(m + 1) * H], ACT.Copy,
                                                   scale=xt[:, qi % 2, ti, FIRST[g] + m:FIRST[g] + m + 1])
                    ins.then_inc(act_step, 1)

            def keep_g(bt, tau):
                act.wait_ge(g_summed, TILES * bt + tau + 2)
                src = ps_g[:, 0:(F + 1) * TB].rearrange("p (j b) -> p j b", b=TB)
                nc.scalar.copy(g_all[:, :, bass.ds(P * bt + TB * tau, TB)], src).then_inc(g_kept, 1)

            def block_scales(bt, last):
                for tau in range(TILES):
                    qi, ti = tau // QT, tau % QT
                    q = QUADS * bt + qi
                    nxt = not (last and qi == QUADS - 1)
                    if ti == 0:
                        act.wait_ge(xt_made, q + 1)
                    scale_groups(bt, qi, ti)
                    if tau >= 1:
                        keep_g(bt, tau - 1)
                    if ti == 1 and nxt:
                        act.wait_ge(dve_step, DVE_STEPS * (QT * q + 1))
                        keep_xt(q + 1, (qi + 1) % 2)
                    if ti == 2 and qi < QUADS - 1:
                        act.wait_ge(y_made, GROUPS * QT * q + 1)
                        keep_x1(q + 1, (qi + 1) % 2)
                    if qi == QUADS - 2 and ti >= 2 and not last:
                        act.wait_ge(z_made, CHUNKS * QUADS * (bt + 1))
                        keep_x0(bt + 1, 2 * (ti - 2))
                        keep_x0(bt + 1, 2 * (ti - 2) + 1)
                if not last:
                    act.wait_ge(y_made, GROUPS * QT * (QUADS * bt + QUADS - 1) + 1)
                    keep_x1(QUADS * (bt + 1), 0)
                keep_g(bt, TILES - 1)

            with act.Fori(0, BLOCKS - 1) as bt:
                block_scales(bt, False)
            block_scales(BLOCKS - 1, True)

            act.wait_ge(bsum_made, 1)
            act.wait_ge(r3_summed, 1)
            nc.scalar.activation(r3[:], ps_x1[:], ACT.Identity, bias=b02_sum[:, 1:2]).then_inc(r3_made, 1)
            for m in range(MC1):
                act.wait_ge(h1_summed, m + 1)
                nc.scalar.activation(h1[:, m, :], ps_y[:, m, :], ACT.Relu, bias=bt1[:, m:m + 1]).then_inc(h1_made, 1)
            for m in range(MC2):
                act.wait_ge(h2_summed, m + 1)
                src = ps_y[:, YBANKS - 1, :] if m == 0 else ps_g[:]
                nc.scalar.activation(h2[:, m, :], src, ACT.Relu, bias=bt2[:, m:m + 1]).then_inc(h2_made, 1)
            act.wait_ge(y_summed, 1)
            nc.scalar.copy(y_row[0:1, :], ps_tr[0:1, :]).then_inc(y_out, 1)

        @block.vector
        def _(dve):
            dve.wait_ge(ident_made, 1)
            nc.vector.tensor_reduce(mask[:], ident[:].rearrange("p (m c) -> p c m", c=TB), AX_X,
                                    ALU.add).then_inc(mask_made, 1)
            dve.wait_ge(mask_made, 1)
            for par in range(2):
                ins = nc.vector.tensor_copy(bd[:, par, :, F, :], mask[:, None, :].broadcast_to([P, QT, TB]))
            ins.then_inc(ones_made, 1)
            dve.wait_ge(w0_ld, 16)
            step = F + 1
            ins = nc.vector.tensor_copy(w0_sym[:, 0:F], w0_in[:, 0:step * (F - 1) + 1:step])
            for s in range(1, SHIFTS):
                n = F - s
                o = s * F
                nc.vector.tensor_tensor(w0_sym[:, o:o + n], w0_in[:, s:s + step * (n - 1) + 1:step],
                                        w0_in[:, F * s:F * s + step * (n - 1) + 1:step], ALU.add)
                a = step * n + s - F
                b = step * n + F * s - F * F
                ins = nc.vector.tensor_tensor(w0_sym[:, o + n:o + F], w0_in[:, a:a + step * (s - 1) + 1:step],
                                              w0_in[:, b:b + step * (s - 1) + 1:step], ALU.add)
            ins.then_inc(w0_summed, 1)
            for n in range(PREP_W1):
                dve.wait_ge(prep_act, n + 1)
                cols = slice(FIRST[n] * H, (FIRST[n] + SIZES[n]) * H)
                nc.vector.tensor_tensor(w1_lo[:, cols], ps_y[:, n % YBANKS, 0:SIZES[n] * H],
                                        w1_hi[:, cols], ALU.subtract).then_inc(prep_dve, 1)

            def multiply(q, par, qi, chunks):
                for c in chunks:
                    r = chunk_rows(c)
                    nc.vector.tensor_tensor(bz[0:r, par, c, :], bz[0:r, par, c, :],
                                            x0[0:r, qi * QN:(qi + 1) * QN], ALU.mult).then_inc(z_made, 1)

            def spread(q, par):
                dve.wait_ge(xt_made, q + 1)
                src = ps_tr[:, 0:QT * (F + 1)].rearrange("p (t j) -> p t j", t=QT)[:, :, 0:F]
                nc.vector.tensor_tensor(bd[:, par, :, 0:F, :],
                                        src[:, :, :, None].broadcast_to([P, QT, F, TB]),
                                        mask[:, None, None, :].broadcast_to([P, QT, F, TB]),
                                        ALU.mult).then_inc(bd_made, 1)

            def split_x1(q, par):
                dve.wait_ge(x1_hi_made, q + 1)
                nc.vector.tensor_reduce(r1[:, bass.ds(QT * TB * q, QT * TB)].rearrange("p (t b) -> p t b", b=TB),
                                        ps_x1[:].rearrange("p (t d b) -> p t b d", d=D, b=TB), AX_X, ALU.add)
                nc.vector.scalar_tensor_tensor(out=x1_lo[:, par, :], in0=ps_x1[:], scalar=b0_col[:, 0:1],
                                               in1=x1_hi[:, par, :], op0=ALU.add,
                                               op1=ALU.subtract).then_inc(x1_lo_made, 1)

            def repeat_rows(bt):
                dve.wait_ge(gathered, 16 * F * (bt + 1))
                rows = emb[:].rearrange("p r f d -> p r (f d)")
                nc.vector.tensor_copy(rows[:, 1:SPC], rows[:, 0:1].broadcast_to([P, SPC - 1, F * D])).then_inc(emb_made, 1)

            repeat_rows(0)
            dve.wait_ge(small_ld, 16 * 7)
            spread(0, 0)
            dve.wait_ge(shifted[0], 16 * SHIFTS)
            multiply(0, 0, 0, range(CHUNKS))
            split_x1(0, 0)
            dve.sem_inc(dve_step, DVE_STEPS)
            dve.sem_inc(join_step, 2 * JOIN_STEPS)

            def join(bt, tau, step):
                T = TILES * bt + tau
                par = tau % 2
                n = JOIN_STEPS * (T + 2)
                s = part[:, par, :]
                wide = ACT_STEPS - POOLED
                if step == 0:
                    dve.wait_ge(pool_step, POOL_STEPS * (T + 2))
                else:
                    dve.wait_ge(join_step, n + step)
                if step < wide:
                    dve.wait_ge(act_step, ACT_STEPS * (T + 1) + POOLED + step + 1)
                    ins = nc.vector.tensor_tensor(s, s, prod[:, POOLED + step, :], ALU.add)
                elif step == wide:
                    ins = nc.vector.tensor_tensor(s[:, 0:2 * H], s[:, 0:2 * H], s[:, 2 * H:4 * H], ALU.add)
                elif step == wide + 1:
                    ins = nc.vector.tensor_tensor(s[:, 0:H], s[:, 0:H], s[:, H:2 * H], ALU.add)
                elif step == wide + 2:
                    dve.wait_ge(dve_step, DVE_STEPS * (T + 2))
                    ins = nc.vector.tensor_tensor(s[:, 0:H], s[:, 0:H], acc[:, par, 0, :], ALU.add)
                else:
                    dve.wait_ge(g_summed, T + 1 if tau == 0 else T)
                    ins = nc.vector.tensor_tensor(x2[:, par, :], s[:, 0:H], acc[:, par, 1, :], ALU.add)
                ins.then_inc(join_step, 1)

            def scale_and_sum(bt, tau, extra=(), rows_of=None):
                qi, ti = tau // QT, tau % QT
                T = TILES * bt + tau
                n = DVE_STEPS * (T + 1)
                done = 0
                joined = 0 if tau else JOIN_STEPS
                for g in DVE_GROUPS:
                    dve.wait_ge(y_made, GROUPS * T + g + 2)
                    for m in range(SIZES[g]):
                        j = FIRST[g] + m
                        a = acc[:, tau % 2, done % 2, :]
                        y = ps_y[:, g % YBANKS, m * H:(m + 1) * H]
                        x = xt[:, qi % 2, ti, j:j + 1]
                        dve.wait_ge(dve_step, n + done - 1)
                        if done == 1:
                            ins = nc.vector.tensor_scalar(a, y, x, None, ALU.mult)
                        else:
                            ins = nc.vector.scalar_tensor_tensor(
                                out=a, in0=y, scalar=x, in1=b1_row[:] if done == 0 else a,
                                op0=ALU.mult, op1=ALU.add)
                        ins.then_inc(dve_step, 1)
                        done += 1
                        if g >= DVE_GROUPS[1] and joined < JOIN_STEPS:
                            join(bt, tau - 1, joined)
                            joined += 1
                    if g == DVE_GROUPS[2] and extra:
                        multiply(*extra)
                    if g == DVE_GROUPS[2] and rows_of is not None:
                        repeat_rows(rows_of)

            def block_sums(bt, last):
                for tau in range(TILES):
                    qi, ti = tau // QT, tau % QT
                    q = QUADS * bt + qi
                    nq, npar = (qi + 1) % QUADS, (qi + 1) % 2
                    nxt = not (last and qi == QUADS - 1)
                    late_q = 1 if qi == QUADS - 1 else 0
                    if ti == 0:
                        dve.wait_ge(xt_made, q + 1)
                    if ti == 2 and not late_q:
                        scale_and_sum(bt, tau, (q + 1, npar, nq, range(5, CHUNKS)),
                                      bt + 1 if qi == QUADS - 2 and not last else None)
                    else:
                        scale_and_sum(bt, tau)
                    if tau == TILES - 1:
                        for step in range(JOIN_STEPS):
                            join(bt, tau, step)
                    if nxt and ti == late_q:
                        dve.wait_ge(shifted[npar], 16 * SHIFTS * (2 * bt + (qi + 1) // 2 + 1))
                        multiply(q + 1, npar, nq, range(0, 3))
                    if nxt and ti == late_q + 1:
                        multiply(q + 1, npar, nq, range(3, CHUNKS if late_q else 5))
                    if nxt and ti == 1:
                        dve.wait_ge(g_summed, QT * q + 1)
                        spread(q + 1, npar)
                    if nxt and ti == (3 if late_q else 2):
                        split_x1(q + 1, npar)

            with dve.Fori(0, BLOCKS - 1) as bt:
                block_sums(bt, False)
            block_sums(BLOCKS - 1, True)
            dve.wait_ge(bsum_made, 1)
            dve.wait_ge(x1_lo_made, BLOCKS * QUADS)
            nc.vector.tensor_scalar(r1[:], r1[:], b02_sum[:, 0:1], None, ALU.add).then_inc(r1_done, 1)

        @block.tensor
        def _(pe):
            def turn_embeddings(bt, s):
                for m in range(PER_SET):
                    src = emb[:].rearrange("p r f d -> p (r f) d")[:, :, PER_SET * s + m]
                    ins = nc.tensor.transpose(ps_tr[0:REP, m * P:(m + 1) * P], src, ident[:])
                ins.then_inc(emb_turned, 1)

            def turn_x(qi):
                for t in range(QT):
                    n = (qi * QT + t) * P
                    ins = nc.tensor.transpose(ps_tr[:, t * (F + 1):t * (F + 1) + F], x0[0:F, n:n + P],
                                              ident[0:F, 0:F])
                ins.then_inc(xt_turned, 1)

            def layer0(q, par, chunks):
                for c in chunks:
                    r = chunk_rows(c)
                    pe.wait_ge(z_made, CHUNKS * q + c + 1)
                    ins = nc.tensor.matmul(ps_x1[:], w0t[0:r, c, :], bz[0:r, par, c, :],
                                           start=c == 0, stop=c == CHUNKS - 1)
                if c == CHUNKS - 1:
                    ins.then_inc(x1_summed, 1)

            for counter in (x1_summed, y_made, g_summed):
                pe.sem_inc(counter, 1)
            pe.wait_ge(ident_made, 1)
            for n in range(PREP):
                if n >= YBANKS:
                    pe.wait_ge(prep_act, n - YBANKS + 1)
                    if n - YBANKS < PREP_W1:
                        pe.wait_ge(prep_dve, n - YBANKS + 1)
                bank = ps_y[:, n % YBANKS, :]
                if n < PREP_W1 + PREP_W2:
                    if n == 0:
                        pe.wait_ge(w1_ld, 16)
                    if n == PREP_W1:
                        pe.wait_ge(w2_ld, 16)
                    g = n % GROUPS
                    src = w1_in if n < PREP_W1 else w2_in
                    for m in range(SIZES[g]):
                        j = FIRST[g] + m
                        ins = nc.tensor.transpose(bank[:, m * H:(m + 1) * H], src[:, j * H:(j + 1) * H], ident[:])
                elif n < PREP - 1:
                    pe.wait_ge(w0_summed, 1)
                    c0 = 4 * (n - PREP_W1 - PREP_W2)
                    for c in range(c0, min(c0 + 4, CHUNKS)):
                        r = chunk_rows(c)
                        ins = nc.tensor.transpose(bank[0:r, (c - c0) * H:(c - c0 + 1) * H],
                                                  w0_sym[:, c * REP:c * REP + r], ident[:])
                else:
                    pe.wait_ge(small_ld, 16 * 7)
                    for c in range(BLOCKS):
                        ins = nc.tensor.transpose(bank[0:C, c * P:(c + 1) * P], dense_sb[:, c, :], ident[:])
                ins.then_inc(prep_tr, 1)

            pe.wait_ge(emb_made, 1)
            for s in range(SETS):
                if s:
                    pe.wait_ge(x0_made, s)
                turn_embeddings(0, s)
            pe.wait_ge(x0_made, SETS)
            turn_x(0)
            pe.wait_ge(prep_act, PREP)
            layer0(0, 0, range(CHUNKS))
            pe.wait_ge(prep_dve, PREP_W1)

            def layer1(bt, qi, ti):
                T = TILES * bt + QT * qi + ti
                n = slice(ti * P, (ti + 1) * P)
                for g in range(GROUPS):
                    before, t = (g - YBANKS, T) if g >= YBANKS else (g + YBANKS, T - 1)
                    if KIND[before] == "D":
                        pe.wait_ge(dve_step, DVE_STEPS * (t + 1) + DVE_DONE[before])
                    else:
                        pe.wait_ge(act_step, ACT_STEPS * (t + 1) + ACT_GROUPS.index(before) + 1)
                    cols = slice(FIRST[g] * H, (FIRST[g] + SIZES[g]) * H)
                    y = ps_y[:, g % YBANKS, 0:SIZES[g] * H]
                    hi, lo = x1_hi[:, qi % 2, n], x1_lo[:, qi % 2, n]
                    nc.tensor.matmul(y, hi, w1_hi[:, cols], start=True, stop=False)
                    nc.tensor.matmul(y, hi, w1_lo[:, cols], start=False, stop=False)
                    nc.tensor.matmul(y, lo, w1_hi[:, cols], start=False, stop=True).then_inc(y_made, 1)

            def sum_d(bt, tau):
                T = TILES * bt + tau
                qi, ti = tau // QT, tau % QT
                pe.wait_ge(join_step, JOIN_STEPS * (T + 3))
                pe.wait_ge(bd_made, QUADS * bt + qi + 1)
                pe.wait_ge(g_kept, T + 1)
                nc.tensor.matmul(ps_g[:, 0:(F + 1) * TB], x2[:, tau % 2, :],
                                 bd[:, qi % 2, ti].rearrange("p j b -> p (j b)"),
                                 start=True, stop=True).then_inc(g_summed, 1)

            def block_products(bt, last):
                for tau in range(TILES):
                    qi, ti = tau // QT, tau % QT
                    q = QUADS * bt + qi
                    nxt = not (last and qi == QUADS - 1)
                    if ti == 0:
                        pe.wait_ge(x1_lo_made, q + 1)
                    layer1(bt, qi, ti)
                    if ti == 1 and nxt:
                        pe.wait_ge(xt_made, q + 1)
                        pe.wait_ge(bd_made, q + 1)
                        pe.wait_ge(x0_made, SETS * (bt + (2 if qi == QUADS - 1 else 1)))
                    if tau >= 1:
                        sum_d(bt, tau - 1)
                    if ti == 1 and nxt:
                        turn_x((qi + 1) % QUADS)
                    if nxt and qi < QUADS - 1 and ti in (1, 2):
                        if ti == 1:
                            pe.wait_ge(x1_lo_made, q + 1)
                        layer0(q + 1, (qi + 1) % 2, range(0, 3) if ti == 1 else range(3, CHUNKS))
                    if qi == QUADS - 2 and ti >= 2 and not last:
                        for s in (2 * (ti - 2), 2 * (ti - 2) + 1):
                            if s == 0:
                                pe.wait_ge(emb_made, bt + 2)
                                pe.wait_ge(xt_made, q + 2)
                                pe.wait_ge(bd_made, q + 2)
                            else:
                                pe.wait_ge(x0_made, SETS * (bt + 1) + s)
                            turn_embeddings(bt + 1, s)
                if not last:
                    pe.wait_ge(x1_lo_made, QUADS * (bt + 1))
                    layer0(QUADS * (bt + 1), 0, range(CHUNKS))
                sum_d(bt, TILES - 1)

            with pe.Fori(0, BLOCKS - 1) as bt:
                block_products(bt, False)
            block_products(BLOCKS - 1, True)

            def mlp1(c, rows, z, start, stop):
                for m in range(MC1):
                    ins = nc.tensor.matmul(ps_y[:, m, :], wt1[0:rows, c, m * P:(m + 1) * P], z,
                                           start=start, stop=stop)
                    if stop:
                        ins.then_inc(h1_summed, 1)

            pe.wait_ge(late_mlp, 64)
            pe.wait_ge(r1_done, 1)
            pe.wait_ge(act_step, ACT_STEPS * (BLOCKS * TILES + 1))
            pe.wait_ge(dve_step, DVE_STEPS * (BLOCKS * TILES + 1))
            mlp1(0, P, r1[:], True, False)
            mlp1(3, C, dense_t, False, False)
            pe.wait_ge(late_w2, 16)
            pe.wait_ge(g_kept, BLOCKS * TILES + 1)
            mlp1(1, P, g_all[:, F, :], False, False)
            for j in range(F):
                ins = nc.tensor.matmul(ps_x1[:], w2t[:, j * H:(j + 1) * H], g_all[:, j, :],
                                       start=j == 0, stop=j == F - 1)
            ins.then_inc(r3_summed, 1)
            pe.wait_ge(r3_made, 1)
            mlp1(2, P, r3[:], False, True)
            for m in range(MC2):
                dst = ps_y[:, YBANKS - 1, :] if m == 0 else ps_g[:]
                for c in range(MC1):
                    if m == 0:
                        pe.wait_ge(h1_made, c + 1)
                    ins = nc.tensor.matmul(dst, wt2[:, c, m * P:(m + 1) * P], h1[:, c, :],
                                           start=c == 0, stop=c == MC1 - 1)
                ins.then_inc(h2_summed, 1)
            for m in range(MC2):
                pe.wait_ge(h2_made, m + 1)
                ins = nc.tensor.matmul(ps_tr[0:1, :], wt3[:, m:m + 1], h2[:, m, :], start=m == 0, stop=m == MC2 - 1)
            ins.then_inc(y_summed, 1)


_TABLES = [f"tbl_{f}" for f in range(F)]
_REST = ["W_top1", "b_top1", "W_top2", "b_top2", "W_top3", "L0_rec_W0", "L0_rec_b0", "L0_rec_W1", "L0_rec_b1",
         "L0_rec_W2", "L0_rec_b2"]


def kernel(**inputs):
    import numpy as _np
    import concourse.bacc as _bacc
    from concourse import mybir as _mybir
    from concourse.bass_utils import run_bass_kernel_spmd as _run

    nc = _bacc.Bacc("TRN2", target_bir_lowering=False, num_devices=1)
    arrays, aps = {}, {}
    for name in ["dense_ctx", "ids"] + _TABLES + _REST:
        a = _np.ascontiguousarray(inputs[name])
        arrays[f"in_{name}"] = a
        aps[name] = nc.dram_tensor(f"in_{name}", a.shape, _mybir.dt.from_np(a.dtype), kind="ExternalInput").ap()
    out = nc.dram_tensor("out_y", (B, 1), F32, kind="ExternalOutput").ap()
    build(nc, aps["dense_ctx"], aps["ids"], [aps[t] for t in _TABLES], *[aps[n] for n in _REST], out)
    r = _run(nc, [arrays], core_ids=[0])
    return r.results[0]["out_y"]
```

```python
from contextlib import ExitStack

import concourse.bass as bass
from concourse import mybir

ALU = mybir.AluOpType
ACT = mybir.ActivationFunctionType
AX_X = mybir.AxisListType.X
F32 = mybir.dt.float32
F32R = mybir.dt.float32r
I32 = mybir.dt.int32

P = 128
B = 512
F = 39
D = 16
H = 128
TB = P // D
TILES = B // TB
QT = 4
QB = QT * TB
QN = QT * P
QUADS = TILES // QT
PAIRS = QUADS // 2
SHIFTS = (F + 1) // 2
SPC = 3
CHUNKS = -(-SHIFTS // SPC)
REP = SPC * F
FPG = P // QB
GATHERS = -(-F // FPG)

SIZES = [4] * 9 + [3]
FIRST = [sum(SIZES[:g]) for g in range(len(SIZES))]
GROUPS = len(SIZES)
YBANKS = 5
KIND = "ADAADADAAD"
DVE_GROUPS = [g for g in range(GROUPS) if KIND[g] == "D"]
ACT_GROUPS = [g for g in range(GROUPS) if KIND[g] == "A"]
POOLED = 4
DVE_STEPS = sum(SIZES[g] for g in DVE_GROUPS)
DVE_DONE = {g: sum(SIZES[x] for x in DVE_GROUPS if x <= g) for g in DVE_GROUPS}
ACT_STEPS = len(ACT_GROUPS)
POOL_STEPS = POOLED - 1
JOIN_STEPS = ACT_STEPS - POOLED + 4
JOINED_AFTER = dict(zip(DVE_GROUPS, ([0, 1], [2, 3], [4, 5])))
GATHERED_IN = [range(0, 4), range(4, 8), range(8, GATHERS), range(0)]
MULTIPLIED_AFTER = {(2, 4): [0, 1], (2, 6): [2], (2, 9): [3], (3, 1): [4, 5], (3, 4): [6]}
SUMMED_AFTER = {(2, 9): [0, 1], (3, 4): [2, 3], (3, 7): [4, 5, 6]}

PREP_W1 = GROUPS
PREP_W2 = GROUPS
PREP_W0 = 2
PREP = PREP_W1 + PREP_W2 + PREP_W0 + 1


def wait(engine, semaphore, value):
    if not isinstance(value, int) or value > 0:
        engine.wait_ge(semaphore, value)


def gather_rows(g):
    return QB * min(FPG, F - FPG * g)


def chunk_rows(c):
    return F * min(SPC, SHIFTS - SPC * c)


def build(nc, dense_ctx, ids, bases, table, W_top1, b_top1, W_top2, b_top2, W_top3, W0, b0, W1, b1, W2, b2, out):
    K1 = W_top1.shape[0]
    M1 = W_top1.shape[1]
    M2 = W_top2.shape[1]
    C = dense_ctx.shape[1]
    MC1, MC2 = M1 // P, M2 // P
    w2t_dram = nc.dram_tensor("w2t_dram", (P, F * H), F32, kind="Internal").ap()
    dense_t_dram = nc.dram_tensor("dense_t_dram", (C, B), F32, kind="Internal").ap()

    with ExitStack() as ctx:
        def sb(name, shape, dt=F32):
            return ctx.enter_context(nc.sbuf_tensor(name, shape, dt))

        def sem(name):
            return ctx.enter_context(nc.semaphore(name))

        ps_y = ctx.enter_context(nc.psum_tensor("ps_y", [P, YBANKS, 512], F32))
        ps_x1 = ctx.enter_context(nc.psum_tensor("ps_x1", [P, 512], F32))
        ps_tr = ctx.enter_context(nc.psum_tensor("ps_tr", [P, 512], F32))
        ps_g = ctx.enter_context(nc.psum_tensor("ps_g", [P, 512], F32))

        w1_hi = sb("w1_hi", [P, F * H], F32R)
        w1_lo = sb("w1_lo", [P, F * H], F32R)
        w0t = sb("w0t", [P, CHUNKS, H])
        g_all = sb("g_all", [P, F + 1, B])
        x0 = sb("x0", [P, 2, QN])
        bz = sb("bz", [P, 2, CHUNKS, QN])
        ids_raw = sb("ids_raw", [P, 2, GATHERS], I32)
        base = sb("base", [P, GATHERS], I32)
        index = sb("index", [P, 2, GATHERS], I32)
        rows = sb("rows", [P, 2, GATHERS, D])
        emb_room = sb("emb_room", [P, 2048])
        emb = emb_room[0:QB, 0:REP * D].rearrange("p (r f d) -> p r f d", r=SPC, d=D)
        ident = sb("ident", [P, P])
        mask = sb("mask", [P, TB])
        x1_hi = sb("x1_hi", [P, 2, QN], F32R)
        x1_lo = sb("x1_lo", [P, 2, QN], F32R)
        xt = sb("xt", [P, 2, QT, F])
        bd = sb("bd", [P, 2, QT, F + 1, TB])
        prod = sb("prod", [P, ACT_STEPS, 4 * H])
        part = sb("part", [P, 2, 4 * H])
        acc = sb("acc", [P, 2, 2, H])
        x2 = sb("x2", [P, 2, H])
        r1 = sb("r1", [P, B])
        r3 = w0t[:].rearrange("p c h -> p (c h)")[:, 0:B]
        dense_sb = sb("dense_sb", [P, B // P, C])
        b1_row = sb("b1_row", [P, H])
        b0_col = sb("b0_col", [P, 1])
        b2_col = sb("b2_col", [P, 1])
        b02_sum = sb("b02_sum", [P, 2])
        bt1 = sb("bt1", [P, MC1])
        bt2 = sb("bt2", [P, MC2])
        wt3 = sb("wt3", [P, MC2])
        y_row = part[:, 0, :]

        flat_g = g_all[:].rearrange("p j b -> p (j b)")
        w1_in = flat_g[:, 0:F * H]
        w2_in = flat_g[:, F * H:2 * F * H]
        w2_out = flat_g[:, 2 * F * H:3 * F * H]
        dense_out = flat_g[0:C, 3 * F * H:3 * F * H + B]
        w0_in = flat_g[:, 3 * F * H + B:3 * F * H + B + F * F]
        w0_sym = bz[:].rearrange("p a c n -> p (a c n)")[:, CHUNKS * QN:CHUNKS * QN + SHIFTS * F]
        late = bz[:].rearrange("p a c n -> p (a c n)")
        w2t = late[:, 0:F * H]
        dense_t = late[0:C, F * H:F * H + B]
        wt2 = x0[:].rearrange("p a n -> p (a n)").rearrange("p (c m) -> p c m", c=MC1)
        wt1 = emb_room[:].rearrange("p (c m) -> p c m", m=M1)
        h1 = g_all
        h2 = g_all[:, MC1:MC1 + MC2, :]

        ids_ld = [sem("ids_ld_0"), sem("ids_ld_1")]
        gathered = [sem("gathered_0"), sem("gathered_1")]
        base_ld, index_made = sem("base_ld"), sem("index_made")
        w0_ld, w1_ld, w2_ld, small_ld = sem("w0_ld"), sem("w1_ld"), sem("w2_ld"), sem("small_ld")
        ident_zero, ident_made = sem("ident_zero"), sem("ident_made")
        mask_made = sem("mask_made")
        w0_summed = sem("w0_summed")
        bsum_made = sem("bsum_made")
        ones_made = sem("ones_made")
        prep_tr, prep_act, prep_dve = sem("prep_tr"), sem("prep_act"), sem("prep_dve")
        w2_saved = sem("w2_saved")
        laid_out = sem("laid_out")
        emb_made = sem("emb_made")
        emb_turned, x0_made = sem("emb_turned"), sem("x0_made")
        shifted = [sem("shifted_0"), sem("shifted_1")]
        z_made, x1_summed = sem("z_made"), sem("x1_summed")
        x1_hi_made, x1_lo_made = sem("x1_hi_made"), sem("x1_lo_made")
        xt_turned, xt_made, bd_made = sem("xt_turned"), sem("xt_made"), sem("bd_made")
        y_made = sem("y_made")
        dve_step, act_step, pool_step = sem("dve_step"), sem("act_step"), sem("pool_step")
        join_step = sem("join_step")
        g_summed, g_kept = sem("g_summed"), sem("g_kept")
        late_w2, late_mlp = sem("late_w2"), sem("late_mlp")
        r1_made = sem("r1_made")
        r1_done, r3_summed, r3_made = sem("r1_done"), sem("r3_summed"), sem("r3_made")
        h1_summed, h1_made = sem("h1_summed"), sem("h1_made")
        h2_summed, h2_made = sem("h2_summed"), sem("h2_made")
        y_summed, y_out, stored = sem("y_summed"), sem("y_out"), sem("stored")

        block = ctx.enter_context(nc.Block())

        @block.sync
        def _(sp):
            def load_ids(q, par):
                sp.dma_start(ids_raw[:, par, :], ids[bass.ds(q * P, P), :]).then_inc(ids_ld[par], 16)

            def lay_out(par):
                for f in range(FPG):
                    n = len(range(f, F, FPG))
                    sp.dma_start(emb[:, 0, f:F:FPG, :], rows[QB * f:QB * (f + 1), par, 0:n, :]).then_inc(laid_out, 16)

            def shift_fields(par):
                for s in range(SHIFTS):
                    lo = (s % SPC) * F
                    sp.dma_start(bz[lo:lo + F, par, s // SPC, :], x0[s:s + F, par, :]).then_inc(shifted[par], 16)

            sp.dma_start(base[:], bases).then_inc(base_ld, 16)
            load_ids(0, 0)
            load_ids(1, 1)
            sp.dma_start(w0_in, W0).then_inc(w0_ld, 16)
            sp.dma_start(w1_in, W1).then_inc(w1_ld, 16)
            for dst, src in ((b0_col[:], b0), (b2_col[:], b2), (bt1[:], b_top1), (bt2[:], b_top2)):
                sp.dma_start(dst, src.rearrange("(c p) -> p c", p=P),
                             allow_slow_non_contiguous=True).then_inc(small_ld, 16)
            sp.dma_start(wt3[:], W_top3.rearrange("(c p) a -> p (c a)", p=P),
                         allow_slow_non_contiguous=True).then_inc(small_ld, 16)
            sp.dma_start(dense_sb[:], dense_ctx.rearrange("(c p) d -> p c d", p=P)).then_inc(small_ld, 16)
            sp.dma_start(b1_row[:], b1.rearrange("(a h) -> a h", a=1).broadcast_to([P, H])).then_inc(small_ld, 16)
            sp.wait_ge(gathered[0], 16 * GATHERS)
            lay_out(0)
            sp.dma_start(w2_in, W2).then_inc(w2_ld, 16)
            sp.wait_ge(x0_made, 1)
            shift_fields(0)
            sp.wait_ge(prep_act, PREP)
            sp.dma_start(w2t_dram, w2_out).then_inc(w2_saved, 16)
            sp.dma_start(dense_t_dram, dense_out).then_inc(w2_saved, 16)

            def pair_loads(i, last):
                for h in range(2):
                    q = 2 * i + h
                    if last and h == 1:
                        continue
                    wait(sp, gathered[1 - h], 16 * GATHERS * (i + 1 + h))
                    lay_out(1 - h)
                    if not last:
                        load_ids(q + 2, h)
                    wait(sp, x1_summed, q)
                    wait(sp, x0_made, q + 2)
                    shift_fields(1 - h)

            pair_loads(0, False)
            with sp.Fori(1, PAIRS - 1) as i:
                pair_loads(i, False)
            pair_loads(PAIRS - 1, True)

            sp.wait_ge(emb_turned, QUADS)
            sp.dma_start(wt1[:, 0:K1 // P, :],
                         W_top1[0:K1 // P * P, :].rearrange("(c p) m -> p c m", p=P)).then_inc(late_mlp, 16)
            sp.dma_start(wt1[0:C, K1 // P, :], W_top1[K1 // P * P:K1, :]).then_inc(late_mlp, 16)
            sp.wait_ge(x1_summed, QUADS)
            sp.wait_ge(w2_saved, 32)
            sp.dma_start(w2t, w2t_dram).then_inc(late_w2, 16)
            sp.dma_start(dense_t, dense_t_dram).then_inc(late_mlp, 16)
            sp.dma_start(wt2, W_top2.rearrange("(c p) m -> p c m", p=P)).then_inc(late_mlp, 16)
            sp.wait_ge(y_out, 1)
            sp.dma_start(out.rearrange("b a -> a b"), y_row[0:1, :]).then_inc(stored, 16)
            sp.wait_ge(stored, 16)

        @block.gpsimd
        def _(pool):
            def make_index(q, par, nth):
                wait(pool, ids_ld[par], 16 * nth)
                nc.gpsimd.tensor_tensor(index[:, par, :], ids_raw[:, par, :], base[:], ALU.add).then_inc(index_made, 1)
                wait(pool, index_made, q + 1)

            def gather(par, g):
                n = gather_rows(g)
                pool.indirect_dma_start(
                    out=rows[0:n, par, g, :], out_offset=None, in_=table,
                    in_offset=bass.IndirectOffsetOnAxis(ap=index[0:n, par, g:g + 1], axis=0),
                ).then_inc(gathered[par], 16)

            pool.wait_ge(base_ld, 16)
            make_index(0, 0, 1)
            for g in range(GATHERS):
                gather(0, g)
            nc.gpsimd.memset(ident[:], 0.0).then_inc(ident_zero, 1)
            pool.wait_ge(ident_zero, 1)
            nc.gpsimd.affine_select(out=ident[:], in_=ident[:], compare_op=ALU.not_equal, fill=1.0, base=0,
                                    pattern=[[-1, P]], channel_multiplier=1).then_inc(ident_made, 1)
            make_index(1, 1, 1)
            for g in range(GATHERS):
                gather(1, g)

            def sum_tile(T, par):
                part_t = part[:, par, :]
                wait(pool, act_step, ACT_STEPS * T + 2)
                wait(pool, join_step, JOIN_STEPS * (T - 1))
                nc.gpsimd.tensor_tensor(part_t, prod[:, 0, :], prod[:, 1, :], ALU.add).then_inc(pool_step, 1)
                for k in range(2, POOLED):
                    wait(pool, act_step, ACT_STEPS * T + k + 1)
                    wait(pool, pool_step, POOL_STEPS * T + k - 1)
                    nc.gpsimd.tensor_tensor(part_t, part_t, prod[:, k, :], ALU.add).then_inc(pool_step, 1)

            def pair_sums(i, last):
                for tau in range(2 * QT):
                    h, ti = tau // QT, tau % QT
                    q = 2 * i + h
                    if ti == 0 and not last:
                        wait(pool, laid_out, 16 * FPG * (q + 1))
                        make_index(q + 2, h, i + 2)
                    sum_tile(2 * QT * i + tau, tau % 2)
                    if last:
                        continue
                    for g in GATHERED_IN[ti]:
                        gather(h, g)

            pair_sums(0, False)
            with pool.Fori(1, PAIRS - 1) as i:
                pair_sums(i, False)
            pair_sums(PAIRS - 1, True)

        @block.scalar
        def _(act):
            def keep_x0(q, par):
                wait(act, z_made, CHUNKS * (q - 1))
                wait(act, emb_turned, q + 1)
                dst = x0[0:REP, par, :].rearrange("p (t d b) -> p d t b", d=D, b=TB)
                src = ps_tr[0:REP].rearrange("p (d t b) -> p d t b", d=D, b=TB)
                nc.scalar.copy(dst, src).then_inc(x0_made, 1)

            def keep_xt(q, par):
                wait(act, dve_step, DVE_STEPS * QT * (q - 1))
                wait(act, xt_turned, q + 1)
                src = ps_tr[:, 0:QT * (F + 1)].rearrange("p (t j) -> p t j", t=QT)[:, :, 0:F]
                nc.scalar.copy(xt[:, par], src).then_inc(xt_made, 1)

            def keep_x1(q, par):
                wait(act, y_made, GROUPS * QT * (q - 1))
                wait(act, x1_summed, q + 1)
                nc.scalar.activation(x1_hi[:, par, :], ps_x1[:], ACT.Identity,
                                     bias=b0_col[:, 0:1]).then_inc(x1_hi_made, 1)

            def keep_prep(n):
                act.wait_ge(prep_tr, n + 1)
                bank = ps_y[:, n % YBANKS, :]
                if n < PREP_W1 + PREP_W2:
                    g = n % GROUPS
                    cols = slice(FIRST[g] * H, (FIRST[g] + SIZES[g]) * H)
                    dst, src = (w1_hi if n < PREP_W1 else w2_out)[:, cols], bank[:, 0:SIZES[g] * H]
                elif n < PREP - 1:
                    c = 4 * (n - PREP_W1 - PREP_W2)
                    full = [x for x in range(c, min(c + 4, CHUNKS)) if chunk_rows(x) == REP]
                    if c + 4 >= CHUNKS:
                        r = chunk_rows(CHUNKS - 1)
                        nc.scalar.copy(w0t[0:r, CHUNKS - 1, :], bank[0:r, len(full) * H:(len(full) + 1) * H])
                    dst = w0t[0:REP, c:c + len(full), :]
                    src = bank[0:REP, 0:len(full) * H].rearrange("p (c h) -> p c h", h=H)
                else:
                    dst, src = dense_out, bank[0:C, :]
                nc.scalar.copy(dst, src).then_inc(prep_act, 1)

            for n in range(PREP):
                keep_prep(n)
            act.wait_ge(small_ld, 16 * 7)
            nc.scalar.mul(b02_sum[:, 0:1], b0_col[:], float(D))
            nc.scalar.mul(b02_sum[:, 1:2], b2_col[:], float(D)).then_inc(bsum_made, 1)

            keep_x0(0, 0)
            keep_xt(0, 0)
            keep_x1(0, 0)

            def scale(T, par, ti, g):
                k = ACT_GROUPS.index(g)
                if k < POOLED:
                    wait(act, pool_step, POOL_STEPS * (T - 1) + max(k, 1))
                else:
                    wait(act, join_step, JOIN_STEPS * (T - 1) + k - POOLED + 1)
                wait(act, y_made, GROUPS * T + g + 1)
                for m in range(SIZES[g]):
                    ins = nc.scalar.activation(prod[:, k, m * H:(m + 1) * H],
                                               ps_y[:, g % YBANKS, m * H:(m + 1) * H], ACT.Copy,
                                               scale=xt[:, par, ti, FIRST[g] + m:FIRST[g] + m + 1])
                ins.then_inc(act_step, 1)

            def keep_g(T):
                if not isinstance(T, int) or T >= 0:
                    wait(act, g_summed, T + 1)
                    src = ps_g[:, 0:(F + 1) * TB].rearrange("p (j b) -> p j b", b=TB)
                    dst = g_all[:, :, T * TB:(T + 1) * TB] if isinstance(T, int) else g_all[:, :, bass.ds(T * TB, TB)]
                    nc.scalar.copy(dst, src).then_inc(g_kept, 1)

            def pair_scales(i, last):
                for tau in range(2 * QT):
                    h, ti = tau // QT, tau % QT
                    q, T = 2 * i + h, 2 * QT * i + tau
                    nxt = not (last and h == 1)
                    if ti == 0:
                        wait(act, xt_made, q + 1)
                    for g in ACT_GROUPS:
                        scale(T, h, ti, g)
                        if g == 3:
                            keep_g(T - 2)
                            if ti == 0 and nxt:
                                keep_x0(q + 1, 1 - h)
                        if g == 5 and ti == 1 and nxt:
                            keep_xt(q + 1, 1 - h)
                        if g == 7 and ti == 3 and nxt:
                            keep_x1(q + 1, 1 - h)

            act.wait_ge(w2_saved, 32)
            pair_scales(0, False)
            with act.Fori(1, PAIRS - 1) as i:
                pair_scales(i, False)
            pair_scales(PAIRS - 1, True)
            keep_g(TILES - 2)
            keep_g(TILES - 1)

            act.wait_ge(bsum_made, 1)
            act.wait_ge(r3_summed, 1)
            nc.scalar.activation(r3, ps_x1[:], ACT.Identity, bias=b02_sum[:, 1:2]).then_inc(r3_made, 1)
            for m in range(MC1):
                act.wait_ge(h1_summed, m + 1)
                nc.scalar.activation(h1[:, m, :], ps_y[:, m, :], ACT.Relu, bias=bt1[:, m:m + 1]).then_inc(h1_made, 1)
            for m in range(MC2):
                act.wait_ge(h2_summed, m + 1)
                src = ps_y[:, YBANKS - 1, :] if m == 0 else ps_g[:]
                nc.scalar.activation(h2[:, m, :], src, ACT.Relu, bias=bt2[:, m:m + 1]).then_inc(h2_made, 1)
            act.wait_ge(y_summed, 1)
            nc.scalar.copy(y_row[0:1, :], ps_tr[0:1, :]).then_inc(y_out, 1)

        @block.vector
        def _(dve):
            dve.wait_ge(ident_made, 1)
            nc.vector.tensor_reduce(mask[:], ident[:].rearrange("p (m c) -> p c m", c=TB), AX_X,
                                    ALU.add).then_inc(mask_made, 1)
            dve.wait_ge(mask_made, 1)
            for par in range(2):
                ins = nc.vector.tensor_copy(bd[:, par, :, F, :], mask[:, None, :].broadcast_to([P, QT, TB]))
            ins.then_inc(ones_made, 1)
            dve.wait_ge(w0_ld, 16)
            step = F + 1
            ins = nc.vector.tensor_copy(w0_sym[:, 0:F], w0_in[:, 0:step * (F - 1) + 1:step])
            for s in range(1, SHIFTS):
                n = F - s
                o = s * F
                nc.vector.tensor_tensor(w0_sym[:, o:o + n], w0_in[:, s:s + step * (n - 1) + 1:step],
                                        w0_in[:, F * s:F * s + step * (n - 1) + 1:step], ALU.add)
                a = step * n + s - F
                b = step * n + F * s - F * F
                ins = nc.vector.tensor_tensor(w0_sym[:, o + n:o + F], w0_in[:, a:a + step * (s - 1) + 1:step],
                                              w0_in[:, b:b + step * (s - 1) + 1:step], ALU.add)
            ins.then_inc(w0_summed, 1)

            def repeat_rows(q):
                wait(dve, laid_out, 16 * FPG * (q + 1))
                flat = emb.rearrange("p r f d -> p r (f d)")
                nc.vector.tensor_copy(flat[:, 1:SPC], flat[:, 0:1].broadcast_to([QB, SPC - 1, F * D])
                                      ).then_inc(emb_made, 1)

            def multiply(par, chunks):
                for c in chunks:
                    r = chunk_rows(c)
                    nc.vector.tensor_tensor(bz[0:r, par, c, :], bz[0:r, par, c, :],
                                            x0[0:r, par, :], ALU.mult).then_inc(z_made, 1)

            def spread(q, par):
                wait(dve, xt_made, q + 1)
                src = ps_tr[:, 0:QT * (F + 1)].rearrange("p (t j) -> p t j", t=QT)[:, :, 0:F]
                nc.vector.tensor_tensor(bd[:, par, :, 0:F, :],
                                        src[:, :, :, None].broadcast_to([P, QT, F, TB]),
                                        mask[:, None, None, :].broadcast_to([P, QT, F, TB]),
                                        ALU.mult).then_inc(bd_made, 1)

            def split_x1(q, par):
                wait(dve, x1_hi_made, q + 1)
                nc.vector.scalar_tensor_tensor(out=x1_lo[:, par, :], in0=ps_x1[:], scalar=b0_col[:, 0:1],
                                               in1=x1_hi[:, par, :], op0=ALU.add,
                                               op1=ALU.subtract).then_inc(x1_lo_made, 1)
                nc.vector.tensor_reduce(r1[:, bass.ds(QB * q, QB)].rearrange("p (t b) -> p t b", b=TB),
                                        ps_x1[:].rearrange("p (t d b) -> p t b d", d=D, b=TB), AX_X,
                                        ALU.add).then_inc(r1_made, 1)

            for n in range(PREP_W1):
                dve.wait_ge(prep_act, n + 1)
                cols = slice(FIRST[n] * H, (FIRST[n] + SIZES[n]) * H)
                nc.vector.tensor_tensor(w1_lo[:, cols], ps_y[:, n % YBANKS, 0:SIZES[n] * H],
                                        w1_hi[:, cols], ALU.subtract).then_inc(prep_dve, 1)
            repeat_rows(0)
            dve.wait_ge(small_ld, 16 * 7)
            spread(0, 0)
            dve.wait_ge(shifted[0], 16 * SHIFTS)
            multiply(0, range(CHUNKS))
            split_x1(0, 0)

            def join(T, par, step):
                s = part[:, par, :]
                wide = ACT_STEPS - POOLED
                if step == 0:
                    wait(dve, pool_step, POOL_STEPS * (T + 1))
                else:
                    wait(dve, join_step, JOIN_STEPS * T + step)
                if step < wide:
                    wait(dve, act_step, ACT_STEPS * T + POOLED + step + 1)
                    ins = nc.vector.tensor_tensor(s, s, prod[:, POOLED + step, :], ALU.add)
                elif step == wide:
                    ins = nc.vector.tensor_tensor(s[:, 0:2 * H], s[:, 0:2 * H], s[:, 2 * H:4 * H], ALU.add)
                elif step == wide + 1:
                    ins = nc.vector.tensor_tensor(s[:, 0:H], s[:, 0:H], s[:, H:2 * H], ALU.add)
                elif step == wide + 2:
                    wait(dve, dve_step, DVE_STEPS * (T + 1))
                    ins = nc.vector.tensor_tensor(s[:, 0:H], s[:, 0:H], acc[:, par, 0, :], ALU.add)
                else:
                    wait(dve, g_summed, T - 1)
                    ins = nc.vector.tensor_tensor(x2[:, par, :], s[:, 0:H], acc[:, par, 1, :], ALU.add)
                ins.then_inc(join_step, 1)

            def scale_and_sum(T, par, h, ti, g):
                wait(dve, y_made, GROUPS * T + g + 1)
                for m in range(SIZES[g]):
                    done = DVE_DONE[g] - SIZES[g] + m
                    a = acc[:, par, done % 2, :]
                    y = ps_y[:, g % YBANKS, m * H:(m + 1) * H]
                    x = xt[:, h, ti, FIRST[g] + m:FIRST[g] + m + 1]
                    wait(dve, dve_step, DVE_STEPS * T + done - 1)
                    if done == 1:
                        ins = nc.vector.tensor_scalar(a, y, x, None, ALU.mult)
                    else:
                        ins = nc.vector.scalar_tensor_tensor(out=a, in0=y, scalar=x,
                                                             in1=b1_row[:] if done == 0 else a,
                                                             op0=ALU.mult, op1=ALU.add)
                    ins.then_inc(dve_step, 1)

            def pair_sums(i, first, last):
                for tau in range(2 * QT):
                    h, ti = tau // QT, tau % QT
                    q, T = 2 * i + h, 2 * QT * i + tau
                    nxt = not (last and h == 1)
                    if ti == 0:
                        wait(dve, xt_made, q + 1)
                        if nxt:
                            repeat_rows(q + 1)
                    for g in DVE_GROUPS:
                        if g == 9 and ti == 3 and nxt:
                            split_x1(q + 1, 1 - h)
                        scale_and_sum(T, tau % 2, h, ti, g)
                        if not (first and tau == 0):
                            for step in JOINED_AFTER.get(g, ()):
                                join(T - 1, (tau - 1) % 2, step)
                        if nxt and (ti, g) in MULTIPLIED_AFTER:
                            if (ti, g) == min(MULTIPLIED_AFTER):
                                wait(dve, shifted[1 - h], 16 * SHIFTS * (i + 1 + h))
                            multiply(1 - h, MULTIPLIED_AFTER[ti, g])
                    if ti == 1 and nxt:
                        wait(dve, g_summed, QT * q)
                        spread(q + 1, 1 - h)

            pair_sums(0, True, False)
            with dve.Fori(1, PAIRS - 1) as i:
                pair_sums(i, False, False)
            pair_sums(PAIRS - 1, False, True)
            for step in range(JOIN_STEPS):
                join(TILES - 1, (TILES - 1) % 2, step)
            dve.wait_ge(bsum_made, 1)
            dve.wait_ge(r1_made, QUADS)
            nc.vector.tensor_scalar(r1[:], r1[:], b02_sum[:, 0:1], None, ALU.add).then_inc(r1_done, 1)

        @block.tensor
        def _(pe):
            def turn_rows():
                flat = emb.rearrange("p r f d -> p (r f) d")
                for d in range(D):
                    ins = nc.tensor.transpose(ps_tr[0:REP, d * QB:(d + 1) * QB], flat[:, :, d], ident[0:QB, 0:QB])
                ins.then_inc(emb_turned, 1)

            def turn_x(par):
                for t in range(QT):
                    ins = nc.tensor.transpose(ps_tr[:, t * (F + 1):t * (F + 1) + F],
                                              x0[0:F, par, t * P:(t + 1) * P], ident[0:F, 0:F])
                ins.then_inc(xt_turned, 1)

            def layer0(q, par, chunks):
                for c in chunks:
                    r = chunk_rows(c)
                    if c == 0:
                        wait(pe, x1_lo_made, q)
                        wait(pe, r1_made, q)
                    wait(pe, z_made, CHUNKS * q + c + 1)
                    ins = nc.tensor.matmul(ps_x1[:], w0t[0:r, c, :], bz[0:r, par, c, :],
                                           start=c == 0, stop=c == CHUNKS - 1)
                if c == CHUNKS - 1:
                    ins.then_inc(x1_summed, 1)

            def turn_prep(n):
                if n >= YBANKS:
                    pe.wait_ge(prep_act, n - YBANKS + 1)
                    if n - YBANKS < PREP_W1:
                        pe.wait_ge(prep_dve, n - YBANKS + 1)
                bank = ps_y[:, n % YBANKS, :]
                if n < PREP_W1 + PREP_W2:
                    if n == 0:
                        pe.wait_ge(w1_ld, 16)
                    if n == PREP_W1:
                        pe.wait_ge(w2_ld, 16)
                    g = n % GROUPS
                    src = w1_in if n < PREP_W1 else w2_in
                    for m in range(SIZES[g]):
                        j = FIRST[g] + m
                        ins = nc.tensor.transpose(bank[:, m * H:(m + 1) * H], src[:, j * H:(j + 1) * H], ident[:])
                elif n < PREP - 1:
                    pe.wait_ge(w0_summed, 1)
                    c0 = 4 * (n - PREP_W1 - PREP_W2)
                    for c in range(c0, min(c0 + 4, CHUNKS)):
                        r = chunk_rows(c)
                        ins = nc.tensor.transpose(bank[0:r, (c - c0) * H:(c - c0 + 1) * H],
                                                  w0_sym[:, c * REP:c * REP + r], ident[:])
                else:
                    pe.wait_ge(small_ld, 16 * 7)
                    for c in range(B // P):
                        ins = nc.tensor.transpose(bank[0:C, c * P:(c + 1) * P], dense_sb[:, c, :], ident[:])
                ins.then_inc(prep_tr, 1)

            pe.wait_ge(ident_made, 1)
            for n in range(PREP):
                turn_prep(n)
            pe.wait_ge(emb_made, 1)
            turn_rows()
            pe.wait_ge(x0_made, 1)
            turn_x(0)
            pe.wait_ge(prep_act, PREP)
            layer0(0, 0, range(CHUNKS))
            pe.wait_ge(prep_dve, PREP_W1)
            pe.wait_ge(ones_made, 1)

            def layer1(T, h, ti, g):
                n = slice(ti * P, (ti + 1) * P)
                before, t = (g - YBANKS, T) if g >= YBANKS else (g + YBANKS, T - 1)
                if KIND[before] == "D":
                    wait(pe, dve_step, DVE_STEPS * t + DVE_DONE[before])
                else:
                    wait(pe, act_step, ACT_STEPS * t + ACT_GROUPS.index(before) + 1)
                cols = slice(FIRST[g] * H, (FIRST[g] + SIZES[g]) * H)
                y = ps_y[:, g % YBANKS, 0:SIZES[g] * H]
                hi, lo = x1_hi[:, h, n], x1_lo[:, h, n]
                nc.tensor.matmul(y, hi, w1_hi[:, cols], start=True, stop=False)
                nc.tensor.matmul(y, hi, w1_lo[:, cols], start=False, stop=False)
                nc.tensor.matmul(y, lo, w1_hi[:, cols], start=False, stop=True).then_inc(y_made, 1)

            def sum_d(T, tau):
                tau = tau % (2 * QT)
                if not isinstance(T, int) or T >= 0:
                    wait(pe, join_step, JOIN_STEPS * (T + 1))
                    wait(pe, bd_made, T // QT + 1 if isinstance(T, int) else 0)
                    wait(pe, g_kept, T)
                    nc.tensor.matmul(ps_g[:, 0:(F + 1) * TB], x2[:, tau % 2, :],
                                     bd[:, tau // QT, tau % QT].rearrange("p j b -> p (j b)"),
                                     start=True, stop=True).then_inc(g_summed, 1)

            def pair_products(i, last):
                for tau in range(2 * QT):
                    h, ti = tau // QT, tau % QT
                    q, T = 2 * i + h, 2 * QT * i + tau
                    nxt = not (last and h == 1)
                    if ti == 0:
                        wait(pe, x1_lo_made, q + 1)
                    for g in range(GROUPS):
                        layer1(T, h, ti, g)
                        if g == 4:
                            wait(pe, bd_made, q + 1)
                            if nxt and ti == 0:
                                wait(pe, emb_made, q + 2)
                            if nxt and ti == 1:
                                wait(pe, x0_made, q + 2)
                            sum_d(T - 2, tau - 2)
                            if nxt and ti == 0:
                                turn_rows()
                            if nxt and ti == 1:
                                turn_x(1 - h)
                        if nxt and (ti, g) in SUMMED_AFTER:
                            layer0(q + 1, 1 - h, SUMMED_AFTER[ti, g])

            pair_products(0, False)
            with pe.Fori(1, PAIRS - 1) as i:
                pair_products(i, False)
            pair_products(PAIRS - 1, True)
            sum_d(TILES - 2, TILES - 2)

            def mlp1(c, rows_c, z, start, stop):
                for m in range(MC1):
                    ins = nc.tensor.matmul(ps_y[:, m, :], wt1[0:rows_c, c, m * P:(m + 1) * P], z,
                                           start=start, stop=stop)
                    if stop:
                        ins.then_inc(h1_summed, 1)

            pe.wait_ge(late_mlp, 64)
            pe.wait_ge(r1_done, 1)
            pe.wait_ge(act_step, ACT_STEPS * TILES)
            pe.wait_ge(dve_step, DVE_STEPS * TILES)
            mlp1(0, P, r1[:], True, False)
            mlp1(3, C, dense_t, False, False)
            sum_d(TILES - 1, TILES - 1)
            pe.wait_ge(late_w2, 16)
            pe.wait_ge(g_kept, TILES)
            mlp1(1, P, g_all[:, F, :], False, False)
            for j in range(F):
                ins = nc.tensor.matmul(ps_x1[:], w2t[:, j * H:(j + 1) * H], g_all[:, j, :],
                                       start=j == 0, stop=j == F - 1)
            ins.then_inc(r3_summed, 1)
            pe.wait_ge(r3_made, 1)
            mlp1(2, P, r3, False, True)
            for m in range(MC2):
                dst = ps_y[:, YBANKS - 1, :] if m == 0 else ps_g[:]
                for c in range(MC1):
                    if m == 0:
                        pe.wait_ge(h1_made, c + 1)
                    ins = nc.tensor.matmul(dst, wt2[:, c, m * P:(m + 1) * P], h1[:, c, :],
                                           start=c == 0, stop=c == MC1 - 1)
                ins.then_inc(h2_summed, 1)
            for m in range(MC2):
                pe.wait_ge(h2_made, m + 1)
                ins = nc.tensor.matmul(ps_tr[0:1, :], wt3[:, m:m + 1], h2[:, m, :], start=m == 0, stop=m == MC2 - 1)
            ins.then_inc(y_summed, 1)


_TABLES = [f"tbl_{f}" for f in range(F)]
_REST = ["W_top1", "b_top1", "W_top2", "b_top2", "W_top3", "L0_rec_W0", "L0_rec_b0", "L0_rec_W1", "L0_rec_b1",
         "L0_rec_W2", "L0_rec_b2"]


def kernel(**inputs):
    import numpy as _np
    import concourse.bacc as _bacc
    from concourse import mybir as _mybir
    from concourse.bass_utils import run_bass_kernel_spmd as _run

    nc = _bacc.Bacc("TRN2", target_bir_lowering=False, num_devices=1)
    table = _np.concatenate([_np.asarray(inputs[t]) for t in _TABLES], axis=0)
    heights = [inputs[t].shape[0] for t in _TABLES]
    ids = _np.zeros((B, GATHERS * FPG), _np.int32)
    ids[:, :F] = _np.asarray(inputs["ids"])
    ids = ids.reshape(QUADS, QB, GATHERS, FPG).transpose(0, 3, 1, 2).reshape(QUADS * P, GATHERS)
    bases = _np.zeros((FPG, QB, GATHERS), _np.int32)
    for f in range(F):
        bases[f % FPG, :, f // FPG] = sum(heights[:f])
    laid_out = {"ids": ids, "bases": bases.reshape(P, GATHERS), "table": table, "dense_ctx": inputs["dense_ctx"]}
    laid_out.update({name: inputs[name] for name in _REST})
    arrays, aps = {}, {}
    for name, a in laid_out.items():
        a = _np.ascontiguousarray(a)
        arrays[f"in_{name}"] = a
        aps[name] = nc.dram_tensor(f"in_{name}", a.shape, _mybir.dt.from_np(a.dtype), kind="ExternalInput").ap()
    out = nc.dram_tensor("out_y", (B, 1), F32, kind="ExternalOutput").ap()
    build(nc, aps["dense_ctx"], aps["ids"], aps["bases"], aps["table"], *[aps[n] for n in _REST], out)
    r = _run(nc, [arrays], core_ids=[0])
    return r.results[0]["out_y"]
```

```python
from contextlib import ExitStack

import concourse.bass as bass
from concourse import mybir

ALU = mybir.AluOpType
ACT = mybir.ActivationFunctionType
AX_X = mybir.AxisListType.X
F32 = mybir.dt.float32
F32R = mybir.dt.float32r
I32 = mybir.dt.int32

P = 128
B = 512
F = 39
D = 16
H = 128
TB = P // D
TILES = B // TB
QT = 4
QB = QT * TB
QN = QT * P
QUADS = TILES // QT
PAIRS = QUADS // 2
SHIFTS = (F + 1) // 2
SPC = 3
CHUNKS = -(-SHIFTS // SPC)
REP = SPC * F
MOVES = SPC + CHUNKS - 1
XROWS = REP + CHUNKS - 1
FPG = P // QB
GATHERS = -(-F // FPG)

SIZES = [4] * 9 + [3]
FIRST = [sum(SIZES[:g]) for g in range(len(SIZES))]
GROUPS = len(SIZES)
YBANKS = 5
KIND = "ADAADADAAD"
DVE_GROUPS = [g for g in range(GROUPS) if KIND[g] == "D"]
ACT_GROUPS = [g for g in range(GROUPS) if KIND[g] == "A"]
POOLED = 4
DVE_STEPS = sum(SIZES[g] for g in DVE_GROUPS)
DVE_DONE = {g: sum(SIZES[x] for x in DVE_GROUPS if x <= g) for g in DVE_GROUPS}
ACT_STEPS = len(ACT_GROUPS)
POOL_STEPS = POOLED - 1
JOIN_STEPS = ACT_STEPS - POOLED + 4
JOINED_AFTER = {(1, 3): 0, (4, 1): 1, (4, 3): 2, (6, 1): 3, (6, 3): 4, (9, 0): 5}
GATHERED_IN = [range(0, 5), range(5, GATHERS), range(0), range(0)]
MULTIPLIED_AFTER = {(0, 9): [0], (1, 1): [1], (1, 4): [2], (1, 9): [3], (2, 4): [4], (2, 6): [5], (2, 9): [6]}
SUMMED_AFTER = {(1, 3): [0], (1, 8): [1], (2, 1): [2], (2, 5): [3], (2, 8): [4], (3, 0): [5], (3, 2): [6]}

HALF = FIRST[GROUPS // 2] * H
W1_PARTS = (slice(0, HALF), slice(HALF, F * H))
PREP_W1 = GROUPS
PREP_W2 = GROUPS
PREP_W0 = 2
PREP = PREP_W1 + PREP_W2 + PREP_W0 + 1


def wait(engine, semaphore, value):
    if not isinstance(value, int) or value > 0:
        engine.wait_ge(semaphore, value)


def gather_rows(g):
    return QB * min(FPG, F - FPG * g)


def chunk_rows(c):
    return F * sum(c + CHUNKS * a < SHIFTS for a in range(SPC))


def pair_runs():
    for c in range(CHUNKS):
        for a in range(chunk_rows(c) // F):
            cuts = sorted({0, F, CHUNKS * a, F - c})
            for j, end in zip(cuts, cuts[1:]):
                yield REP * c + F * a + j, (j - CHUNKS * a) % F, (j + c) % F, end - j


def build(nc, dense_ctx, ids, bases, table, W_top1, b_top1, W_top2, b_top2, W_top3, W0, b0, W1, b1, W2, b2, out):
    K1 = W_top1.shape[0]
    M1 = W_top1.shape[1]
    M2 = W_top2.shape[1]
    C = dense_ctx.shape[1]
    MC1, MC2 = M1 // P, M2 // P
    w2t_dram = nc.dram_tensor("w2t_dram", (P, F * H), F32, kind="Internal").ap()
    dense_t_dram = nc.dram_tensor("dense_t_dram", (C, B), F32, kind="Internal").ap()

    with ExitStack() as ctx:
        def sb(name, shape, dt=F32):
            return ctx.enter_context(nc.sbuf_tensor(name, shape, dt))

        def sem(name):
            return ctx.enter_context(nc.semaphore(name))

        ps_y = ctx.enter_context(nc.psum_tensor("ps_y", [P, YBANKS, 512], F32))
        ps_x1 = ctx.enter_context(nc.psum_tensor("ps_x1", [P, 512], F32))
        ps_tr = ctx.enter_context(nc.psum_tensor("ps_tr", [P, 512], F32))
        ps_g = ctx.enter_context(nc.psum_tensor("ps_g", [P, 512], F32))

        w1_hi = sb("w1_hi", [P, F * H], F32R)
        w1_lo = sb("w1_lo", [P, F * H], F32R)
        w0t = sb("w0t", [P, CHUNKS, H])
        g_all = sb("g_all", [P, F + 1, B])
        x0 = sb("x0", [P, 2, QN])
        xa = sb("xa", [P, QN])
        bz = sb("bz", [P, 2, CHUNKS, QN])
        ids_all = sb("ids_all", [P, QUADS * GATHERS], I32)
        base = sb("base", [P, GATHERS], I32)
        index = sb("index", [P, 2, GATHERS], I32)
        rows = sb("rows", [P, 2, GATHERS, D])
        emb_room = sb("emb_room", [P, 2048])
        emb = emb_room[0:QB, 0:XROWS * D].rearrange("p (f d) -> p f d", d=D)
        ident = sb("ident", [P, P])
        mask = sb("mask", [P, TB])
        x1_hi = sb("x1_hi", [P, 2, QN], F32R)
        x1_lo = sb("x1_lo", [P, 2, QN], F32R)
        xt = sb("xt", [P, 2, QT, F])
        bd = sb("bd", [P, 2, QT, F + 1, TB])
        prod = sb("prod", [P, ACT_STEPS, 4 * H])
        part = sb("part", [P, 2, 4 * H])
        acc = sb("acc", [P, 2, 2, H])
        x2 = sb("x2", [P, 2, H])
        r1 = sb("r1", [P, B])
        r3 = w0t[:].rearrange("p c h -> p (c h)")[:, 0:B]
        b1_row = sb("b1_row", [P, H])
        columns = sb("columns", [P, 4 + MC1 + 2 * MC2])
        b0_col, b2_col = columns[:, 0:1], columns[:, 1:2]
        b02_sum = columns[:, 2:4]
        bt1 = columns[:, 4:4 + MC1]
        bt2 = columns[:, 4 + MC1:4 + MC1 + MC2]
        wt3 = columns[:, 4 + MC1 + MC2:]
        y_row = part[:, 0, :]

        flat_g = g_all[:].rearrange("p j b -> p (j b)")
        w1_in = flat_g[:, 0:F * H]
        w2_in = flat_g[:, F * H:2 * F * H]
        w2_out = flat_g[:, 2 * F * H:3 * F * H]
        dense_out = flat_g[0:C, 3 * F * H:3 * F * H + B]
        w0_in = flat_g[:, 3 * F * H + B:3 * F * H + B + F * F]
        dense_in = flat_g[:, 3 * F * H + B + F * F:3 * F * H + B + F * F + B // P * C].rearrange("p (c d) -> p c d", d=C)
        w0_sym = bz[:].rearrange("p a c n -> p (a c n)")[:, CHUNKS * QN:CHUNKS * QN + SHIFTS * F]
        late = bz[:].rearrange("p a c n -> p (a c n)")
        w2t = late[:, 0:F * H]
        dense_t = late[0:C, F * H:F * H + B]
        wt2 = x0[:].rearrange("p a n -> p (a n)").rearrange("p (c m) -> p c m", c=MC1)
        wt1 = emb_room[:].rearrange("p (c m) -> p c m", m=M1)
        h1 = g_all
        h2 = g_all[:, MC1:MC1 + MC2, :]

        gathered = [sem("gathered_0"), sem("gathered_1")]
        ids_ld, index_made = sem("ids_ld"), sem("index_made")
        w0_ld, w2_ld, small_ld = sem("w0_ld"), sem("w2_ld"), sem("small_ld")
        w1_ld = [sem("w1_ld_0"), sem("w1_ld_1")]
        ident_zero, ident_made = sem("ident_zero"), sem("ident_made")
        mask_made = sem("mask_made")
        w0_summed = sem("w0_summed")
        bsum_made = sem("bsum_made")
        ones_made = sem("ones_made")
        prep_tr, prep_act, prep_dve = sem("prep_tr"), sem("prep_act"), sem("prep_dve")
        w2_saved = sem("w2_saved")
        laid_out = sem("laid_out")
        emb_made = sem("emb_made")
        emb_turned, x0_made = sem("emb_turned"), sem("x0_made")
        shifted = [sem("shifted_0"), sem("shifted_1")]
        first_shared = sem("first_shared")
        first_window = [None] + [sem(f"first_window_{c}") for c in range(1, CHUNKS)]
        z_made, x1_summed = sem("z_made"), sem("x1_summed")
        x1_hi_made, x1_lo_made = sem("x1_hi_made"), sem("x1_lo_made")
        xt_turned, xt_made, bd_made = sem("xt_turned"), sem("xt_made"), sem("bd_made")
        y_made = sem("y_made")
        dve_step, act_step, pool_step = sem("dve_step"), sem("act_step"), sem("pool_step")
        join_step = sem("join_step")
        g_summed, g_kept = sem("g_summed"), sem("g_kept")
        late_w2, late_mlp = sem("late_w2"), sem("late_mlp")
        r1_made = sem("r1_made")
        r1_done, r3_summed, r3_made = sem("r1_done"), sem("r3_summed"), sem("r3_made")
        h1_summed, h1_made = sem("h1_summed"), sem("h1_made")
        h2_summed, h2_made = sem("h2_summed"), sem("h2_made")
        y_summed, y_out, stored = sem("y_summed"), sem("y_out"), sem("stored")

        block = ctx.enter_context(nc.Block())

        @block.sync
        def _(sp):
            def lay_out(par):
                for f in range(FPG):
                    n = len(range(f, F, FPG))
                    sp.dma_start(emb[:, f:F:FPG, :], rows[QB * f:QB * (f + 1), par, 0:n, :]).then_inc(laid_out, 16)

            def share_rows(par, landed):
                for a in range(SPC):
                    at = -CHUNKS * a % F
                    sp.dma_start(xa[F * a:F * (a + 1), :], x0[at:at + F, par, :]).then_inc(landed, 16)

            def cut_window(par, c, landed):
                n = chunk_rows(c)
                sp.dma_start(bz[0:n, par, c, :], x0[c:c + n, par, :]).then_inc(landed, 16)

            def cut_windows(par):
                for c in range(1, CHUNKS):
                    cut_window(par, c, shifted[par])

            sp.dma_start(base[:], bases).then_inc(ids_ld, 16)
            sp.dma_start(ids_all[:], ids).then_inc(ids_ld, 16)
            sp.dma_start(w0_in, W0).then_inc(w0_ld, 16)
            for part_ld, cols in zip(w1_ld, W1_PARTS):
                sp.dma_start(w1_in[:, cols], W1[:, cols]).then_inc(part_ld, 16)
            for dst, src in ((b0_col[:], b0), (b2_col[:], b2), (bt1[:], b_top1), (bt2[:], b_top2)):
                sp.dma_start(dst, src.rearrange("(c p) -> p c", p=P),
                             allow_slow_non_contiguous=True).then_inc(small_ld, 16)
            sp.dma_start(wt3[:], W_top3.rearrange("(c p) a -> p (c a)", p=P),
                         allow_slow_non_contiguous=True).then_inc(small_ld, 16)
            sp.dma_start(dense_in, dense_ctx.rearrange("(c p) d -> p c d", p=P)).then_inc(small_ld, 16)
            sp.dma_start(b1_row[:], b1.rearrange("(a h) -> a h", a=1).broadcast_to([P, H])).then_inc(small_ld, 16)
            sp.wait_ge(gathered[0], 16 * GATHERS)
            lay_out(0)
            sp.dma_start(w2_in, W2).then_inc(w2_ld, 16)
            sp.wait_ge(x0_made, 1)
            share_rows(0, first_shared)
            for c in range(1, CHUNKS):
                cut_window(0, c, first_window[c])
            sp.wait_ge(gathered[1], 16 * GATHERS)
            lay_out(1)
            sp.wait_ge(prep_act, PREP)
            sp.dma_start(w2t_dram, w2_out).then_inc(w2_saved, 16)
            sp.dma_start(dense_t_dram, dense_out).then_inc(w2_saved, 16)
            sp.wait_ge(x0_made, 2)
            sp.wait_ge(prep_tr, PREP_W1 + PREP_W0)
            cut_windows(1)
            sp.wait_ge(z_made, CHUNKS)
            share_rows(1, shifted[1])

            def pair_loads(i):
                for h in range(2):
                    q = 2 * i + h
                    wait(sp, gathered[h], 16 * GATHERS * (i + 2))
                    lay_out(h)
                    wait(sp, x0_made, q + 3)
                    cut_windows(h)
                    wait(sp, z_made, CHUNKS * (q + 2))
                    share_rows(h, shifted[h])

            pair_loads(0)
            with sp.Fori(1, PAIRS - 1) as i:
                pair_loads(i)

            sp.wait_ge(emb_turned, QUADS)
            sp.dma_start(wt1[:, 0:K1 // P, :],
                         W_top1[0:K1 // P * P, :].rearrange("(c p) m -> p c m", p=P)).then_inc(late_mlp, 16)
            sp.dma_start(wt1[0:C, K1 // P, :], W_top1[K1 // P * P:K1, :]).then_inc(late_mlp, 16)
            sp.wait_ge(x1_summed, QUADS)
            sp.wait_ge(w2_saved, 32)
            sp.dma_start(w2t, w2t_dram).then_inc(late_w2, 16)
            sp.dma_start(dense_t, dense_t_dram).then_inc(late_mlp, 16)
            sp.dma_start(wt2, W_top2.rearrange("(c p) m -> p c m", p=P)).then_inc(late_mlp, 16)
            sp.wait_ge(y_out, 1)
            sp.dma_start(out.rearrange("b a -> a b"), y_row[0:1, :]).then_inc(stored, 16)
            sp.wait_ge(stored, 16)

        @block.gpsimd
        def _(pool):
            def make_index(q, par):
                nc.gpsimd.tensor_tensor(index[:, par, :], ids_all[:, bass.ds(q * GATHERS, GATHERS)], base[:],
                                        ALU.add).then_inc(index_made, 1)
                wait(pool, index_made, q + 1)

            def gather(par, g):
                n = gather_rows(g)
                pool.indirect_dma_start(
                    out=rows[0:n, par, g, :], out_offset=None, in_=table,
                    in_offset=bass.IndirectOffsetOnAxis(ap=index[0:n, par, g:g + 1], axis=0),
                ).then_inc(gathered[par], 16)

            nc.gpsimd.memset(ident[:], 0.0).then_inc(ident_zero, 1)
            pool.wait_ge(ident_zero, 1)
            nc.gpsimd.affine_select(out=ident[:], in_=ident[:], compare_op=ALU.not_equal, fill=1.0, base=0,
                                    pattern=[[-1, P]], channel_multiplier=1).then_inc(ident_made, 1)
            pool.wait_ge(ids_ld, 32)
            for q in range(2):
                make_index(q, q)
                for g in range(GATHERS):
                    gather(q, g)

            def sum_tile(T, par):
                part_t = part[:, par, :]
                wait(pool, act_step, ACT_STEPS * T + 2)
                wait(pool, join_step, JOIN_STEPS * (T - 1))
                nc.gpsimd.tensor_tensor(part_t, prod[:, 0, :], prod[:, 1, :], ALU.add).then_inc(pool_step, 1)
                for k in range(2, POOLED):
                    wait(pool, act_step, ACT_STEPS * T + k + 1)
                    wait(pool, pool_step, POOL_STEPS * T + k - 1)
                    nc.gpsimd.tensor_tensor(part_t, part_t, prod[:, k, :], ALU.add).then_inc(pool_step, 1)

            def pair_sums(i, last):
                for tau in range(2 * QT):
                    h, ti = tau // QT, tau % QT
                    q = 2 * i + h
                    if ti == 0 and not last:
                        wait(pool, laid_out, 16 * FPG * (q + 1))
                        make_index(q + 2, h)
                    sum_tile(2 * QT * i + tau, tau % 2)
                    if last:
                        continue
                    for g in GATHERED_IN[ti]:
                        gather(h, g)

            pair_sums(0, False)
            with pool.Fori(1, PAIRS - 1) as i:
                pair_sums(i, False)
            pair_sums(PAIRS - 1, True)

        @block.scalar
        def _(act):
            def keep_x0(q, par):
                wait(act, z_made, CHUNKS * (q - 1))
                wait(act, emb_turned, q + 1)
                dst = x0[0:XROWS, par, :].rearrange("p (t d b) -> p d t b", d=D, b=TB)
                src = ps_tr[0:XROWS].rearrange("p (d t b) -> p d t b", d=D, b=TB)
                nc.scalar.copy(dst, src).then_inc(x0_made, 1)

            def keep_xt(q, par):
                wait(act, dve_step, DVE_STEPS * QT * (q - 1))
                wait(act, xt_turned, q + 1)
                src = ps_tr[:, 0:QT * (F + 1)].rearrange("p (t j) -> p t j", t=QT)[:, :, 0:F]
                nc.scalar.copy(xt[:, par], src).then_inc(xt_made, 1)

            def keep_x1(q, par):
                wait(act, y_made, GROUPS * QT * (q - 1))
                wait(act, x1_summed, q + 1)
                nc.scalar.activation(x1_hi[:, par, :], ps_x1[:], ACT.Identity,
                                     bias=b0_col[:, 0:1]).then_inc(x1_hi_made, 1)

            def keep_prep(n):
                act.wait_ge(prep_tr, n + 1)
                bank = ps_y[:, n % YBANKS, :]
                if n < PREP_W1 or n > PREP_W1 + PREP_W0:
                    g = n if n < PREP_W1 else n - (PREP - PREP_W2)
                    cols = slice(FIRST[g] * H, (FIRST[g] + SIZES[g]) * H)
                    dst, src = (w1_hi if n < PREP_W1 else w2_out)[:, cols], bank[:, 0:SIZES[g] * H]
                elif n < PREP_W1 + PREP_W0:
                    c = 4 * (n - PREP_W1)
                    full = [x for x in range(c, min(c + 4, CHUNKS)) if chunk_rows(x) == REP]
                    if c + 4 >= CHUNKS:
                        r = chunk_rows(CHUNKS - 1)
                        nc.scalar.copy(w0t[0:r, CHUNKS - 1, :], bank[0:r, len(full) * H:(len(full) + 1) * H])
                    dst = w0t[0:REP, c:c + len(full), :]
                    src = bank[0:REP, 0:len(full) * H].rearrange("p (c h) -> p c h", h=H)
                else:
                    dst, src = dense_out, bank[0:C, :]
                nc.scalar.copy(dst, src).then_inc(prep_act, 1)

            for n in range(PREP - PREP_W2):
                keep_prep(n)
            act.wait_ge(small_ld, 16 * 7)
            nc.scalar.mul(b02_sum[:, 0:1], b0_col[:], float(D))
            nc.scalar.mul(b02_sum[:, 1:2], b2_col[:], float(D)).then_inc(bsum_made, 1)
            keep_x0(0, 0)
            keep_xt(0, 0)
            for n in range(PREP - PREP_W2, PREP):
                keep_prep(n)
            keep_x1(0, 0)
            keep_x0(1, 1)

            def scale(T, par, ti, g):
                k = ACT_GROUPS.index(g)
                if k < POOLED:
                    wait(act, pool_step, POOL_STEPS * (T - 1) + max(k, 1))
                else:
                    wait(act, join_step, JOIN_STEPS * (T - 1) + k - POOLED + 1)
                wait(act, y_made, GROUPS * T + g + 1)
                for m in range(SIZES[g]):
                    ins = nc.scalar.activation(prod[:, k, m * H:(m + 1) * H],
                                               ps_y[:, g % YBANKS, m * H:(m + 1) * H], ACT.Copy,
                                               scale=xt[:, par, ti, FIRST[g] + m:FIRST[g] + m + 1])
                ins.then_inc(act_step, 1)

            def keep_g(T):
                if isinstance(T, int) and T == 0:
                    act.wait_ge(w2_saved, 32)
                if not isinstance(T, int) or T >= 0:
                    wait(act, g_summed, T + 1)
                    src = ps_g[:, 0:(F + 1) * TB].rearrange("p (j b) -> p j b", b=TB)
                    dst = g_all[:, :, T * TB:(T + 1) * TB] if isinstance(T, int) else g_all[:, :, bass.ds(T * TB, TB)]
                    nc.scalar.copy(dst, src).then_inc(g_kept, 1)

            def pair_scales(i, last):
                for tau in range(2 * QT):
                    h, ti = tau // QT, tau % QT
                    q, T = 2 * i + h, 2 * QT * i + tau
                    nxt = not (last and h == 1)
                    if ti == 0:
                        wait(act, xt_made, q + 1)
                    for g in ACT_GROUPS:
                        scale(T, h, ti, g)
                        if g == 3:
                            keep_g(T - 2)
                        if g == 8 and ti == 3 and not last:
                            keep_x0(q + 2, h)
                        if g == 5 and ti == 1 and nxt:
                            keep_xt(q + 1, 1 - h)
                        if g == 5 and ti == 3 and nxt:
                            keep_x1(q + 1, 1 - h)

            pair_scales(0, False)
            with act.Fori(1, PAIRS - 1) as i:
                pair_scales(i, False)
            pair_scales(PAIRS - 1, True)
            keep_g(TILES - 2)
            keep_g(TILES - 1)

            act.wait_ge(bsum_made, 1)
            act.wait_ge(r3_summed, 1)
            nc.scalar.activation(r3, ps_x1[:], ACT.Identity, bias=b02_sum[:, 1:2]).then_inc(r3_made, 1)
            for m in range(MC1):
                act.wait_ge(h1_summed, m + 1)
                nc.scalar.activation(h1[:, m, :], ps_y[:, m, :], ACT.Relu, bias=bt1[:, m:m + 1]).then_inc(h1_made, 1)
            for m in range(MC2):
                act.wait_ge(h2_summed, m + 1)
                src = ps_y[:, YBANKS - 1, :] if m == 0 else ps_g[:]
                nc.scalar.activation(h2[:, m, :], src, ACT.Relu, bias=bt2[:, m:m + 1]).then_inc(h2_made, 1)
            act.wait_ge(y_summed, 1)
            nc.scalar.copy(y_row[0:1, :], ps_tr[0:1, :]).then_inc(y_out, 1)

        @block.vector
        def _(dve):
            dve.wait_ge(ident_made, 1)
            nc.vector.tensor_reduce(mask[:], ident[:].rearrange("p (m c) -> p c m", c=TB), AX_X,
                                    ALU.add).then_inc(mask_made, 1)
            dve.wait_ge(mask_made, 1)
            for par in range(2):
                ins = nc.vector.tensor_copy(bd[:, par, :, F, :], mask[:, None, :].broadcast_to([P, QT, TB]))
            ins.then_inc(ones_made, 1)
            dve.wait_ge(w0_ld, 16)
            for row, u, v, n in pair_runs():
                dst = w0_sym[:, row:row + n]
                span = (F + 1) * (n - 1) + 1
                uv = w0_in[:, F * u + v:F * u + v + span:F + 1]
                vu = w0_in[:, F * v + u:F * v + u + span:F + 1]
                ins = nc.vector.tensor_copy(dst, uv) if u == v else nc.vector.tensor_tensor(dst, uv, vu, ALU.add)
            ins.then_inc(w0_summed, 1)

            def repeat_rows(q):
                wait(dve, laid_out, 16 * FPG * (q + 1))
                flat = emb_room[0:QB, :]
                n = F * D
                nc.vector.tensor_copy(flat[:, n:SPC * n].rearrange("p (r n) -> p r n", n=n),
                                      flat[:, None, 0:n].broadcast_to([QB, SPC - 1, n]))
                nc.vector.tensor_copy(flat[:, SPC * n:XROWS * D], flat[:, 0:(XROWS - REP) * D]).then_inc(emb_made, 1)

            def multiply(par, chunks):
                for c in chunks:
                    r = chunk_rows(c)
                    window = bz[0:r, par, c, :] if c else x0[0:r, par, :]
                    nc.vector.tensor_tensor(bz[0:r, par, c, :], window, xa[0:r, :],
                                            ALU.mult).then_inc(z_made, 1)

            def spread(q, par):
                wait(dve, xt_made, q + 1)
                src = ps_tr[:, 0:QT * (F + 1)].rearrange("p (t j) -> p t j", t=QT)[:, :, 0:F]
                nc.vector.tensor_tensor(bd[:, par, :, 0:F, :],
                                        src[:, :, :, None].broadcast_to([P, QT, F, TB]),
                                        mask[:, None, None, :].broadcast_to([P, QT, F, TB]),
                                        ALU.mult).then_inc(bd_made, 1)

            def split_x1(q, par):
                wait(dve, x1_hi_made, q + 1)
                nc.vector.scalar_tensor_tensor(out=x1_lo[:, par, :], in0=ps_x1[:], scalar=b0_col[:, 0:1],
                                               in1=x1_hi[:, par, :], op0=ALU.add,
                                               op1=ALU.subtract).then_inc(x1_lo_made, 1)
                nc.vector.tensor_reduce(r1[:, bass.ds(QB * q, QB)].rearrange("p (t b) -> p t b", b=TB),
                                        ps_x1[:].rearrange("p (t d b) -> p t b d", d=D, b=TB), AX_X,
                                        ALU.add).then_inc(r1_made, 1)

            for n in range(PREP_W1):
                dve.wait_ge(prep_act, n + 1)
                cols = slice(FIRST[n] * H, (FIRST[n] + SIZES[n]) * H)
                nc.vector.tensor_tensor(w1_lo[:, cols], ps_y[:, n % YBANKS, 0:SIZES[n] * H],
                                        w1_hi[:, cols], ALU.subtract).then_inc(prep_dve, 1)
            repeat_rows(0)
            spread(0, 0)
            dve.wait_ge(first_shared, 16 * SPC)
            for c in range(CHUNKS):
                if c > 0:
                    dve.wait_ge(first_window[c], 16)
                multiply(0, [c])
            repeat_rows(1)
            dve.wait_ge(small_ld, 16 * 7)
            split_x1(0, 0)

            def join(T, par, step):
                s = part[:, par, :]
                wide = ACT_STEPS - POOLED
                if step == 0:
                    wait(dve, pool_step, POOL_STEPS * (T + 1))
                else:
                    wait(dve, join_step, JOIN_STEPS * T + step)
                if step < wide:
                    wait(dve, act_step, ACT_STEPS * T + POOLED + step + 1)
                    ins = nc.vector.tensor_tensor(s, s, prod[:, POOLED + step, :], ALU.add)
                elif step == wide:
                    ins = nc.vector.tensor_tensor(s[:, 0:2 * H], s[:, 0:2 * H], s[:, 2 * H:4 * H], ALU.add)
                elif step == wide + 1:
                    ins = nc.vector.tensor_tensor(s[:, 0:H], s[:, 0:H], s[:, H:2 * H], ALU.add)
                elif step == wide + 2:
                    wait(dve, dve_step, DVE_STEPS * (T + 1))
                    ins = nc.vector.tensor_tensor(s[:, 0:H], s[:, 0:H], acc[:, par, 0, :], ALU.add)
                else:
                    wait(dve, g_summed, T - 1)
                    ins = nc.vector.tensor_tensor(x2[:, par, :], s[:, 0:H], acc[:, par, 1, :], ALU.add)
                ins.then_inc(join_step, 1)

            def scale_and_sum(T, par, h, ti, g, alone):
                wait(dve, y_made, GROUPS * T + g + 1)
                for m in range(SIZES[g]):
                    done = DVE_DONE[g] - SIZES[g] + m
                    a = acc[:, par, done % 2, :]
                    y = ps_y[:, g % YBANKS, m * H:(m + 1) * H]
                    x = xt[:, h, ti, FIRST[g] + m:FIRST[g] + m + 1]
                    wait(dve, dve_step, DVE_STEPS * T + done - 1)
                    if done == 1:
                        ins = nc.vector.tensor_scalar(a, y, x, None, ALU.mult)
                    else:
                        ins = nc.vector.scalar_tensor_tensor(out=a, in0=y, scalar=x,
                                                             in1=b1_row[:] if done == 0 else a,
                                                             op0=ALU.mult, op1=ALU.add)
                    ins.then_inc(dve_step, 1)
                    if (g, m) in JOINED_AFTER and not alone:
                        join(T - 1, 1 - par, JOINED_AFTER[g, m])

            def pair_sums(i, first, last):
                for tau in range(2 * QT):
                    h, ti = tau // QT, tau % QT
                    q, T = 2 * i + h, 2 * QT * i + tau
                    nxt = not (last and h == 1)
                    if ti == 0:
                        wait(dve, xt_made, q + 1)
                    for g in DVE_GROUPS:
                        if g == 6 and ti == 3 and nxt:
                            split_x1(q + 1, 1 - h)
                        scale_and_sum(T, tau % 2, h, ti, g, first and tau == 0)
                        if g == 1 and ti == 3 and not last:
                            repeat_rows(q + 2)
                        if nxt and (ti, g) in MULTIPLIED_AFTER:
                            if (ti, g) == min(MULTIPLIED_AFTER):
                                wait(dve, shifted[1 - h], 16 * MOVES * (i + 1))
                            multiply(1 - h, MULTIPLIED_AFTER[ti, g])
                    if ti == 1 and nxt:
                        wait(dve, g_summed, QT * q)
                        spread(q + 1, 1 - h)

            pair_sums(0, True, False)
            with dve.Fori(1, PAIRS - 1) as i:
                pair_sums(i, False, False)
            pair_sums(PAIRS - 1, False, True)
            for step in range(JOIN_STEPS):
                join(TILES - 1, (TILES - 1) % 2, step)
            dve.wait_ge(bsum_made, 1)
            dve.wait_ge(r1_made, QUADS)
            nc.vector.tensor_scalar(r1[:], r1[:], b02_sum[:, 0:1], None, ALU.add).then_inc(r1_done, 1)

        @block.tensor
        def _(pe):
            def turn_rows():
                for d in range(D):
                    ins = nc.tensor.transpose(ps_tr[0:XROWS, d * QB:(d + 1) * QB], emb[:, :, d], ident[0:QB, 0:QB])
                ins.then_inc(emb_turned, 1)

            def turn_x(par):
                for t in range(QT):
                    ins = nc.tensor.transpose(ps_tr[:, t * (F + 1):t * (F + 1) + F],
                                              x0[0:F, par, t * P:(t + 1) * P], ident[0:F, 0:F])
                ins.then_inc(xt_turned, 1)

            def layer0(q, par, chunks):
                for c in chunks:
                    r = chunk_rows(c)
                    if c == 0:
                        wait(pe, x1_lo_made, q)
                        wait(pe, r1_made, q)
                    wait(pe, z_made, CHUNKS * q + c + 1)
                    ins = nc.tensor.matmul(ps_x1[:], w0t[0:r, c, :], bz[0:r, par, c, :],
                                           start=c == 0, stop=c == CHUNKS - 1)
                if c == CHUNKS - 1:
                    ins.then_inc(x1_summed, 1)

            def turn_prep(n):
                if n >= YBANKS:
                    pe.wait_ge(prep_act, n - YBANKS + 1)
                    if n - YBANKS < PREP_W1:
                        pe.wait_ge(prep_dve, n - YBANKS + 1)
                bank = ps_y[:, n % YBANKS, :]
                if n < PREP_W1 or n > PREP_W1 + PREP_W0:
                    if n in (0, GROUPS // 2):
                        pe.wait_ge(w1_ld[n // (GROUPS // 2)], 16)
                    if n == PREP - PREP_W2:
                        pe.wait_ge(w2_ld, 16)
                    g = n if n < PREP_W1 else n - (PREP - PREP_W2)
                    src = w1_in if n < PREP_W1 else w2_in
                    for m in range(SIZES[g]):
                        j = FIRST[g] + m
                        ins = nc.tensor.transpose(bank[:, m * H:(m + 1) * H], src[:, j * H:(j + 1) * H], ident[:])
                elif n < PREP_W1 + PREP_W0:
                    pe.wait_ge(w0_summed, 1)
                    c0 = 4 * (n - PREP_W1)
                    for c in range(c0, min(c0 + 4, CHUNKS)):
                        r = chunk_rows(c)
                        ins = nc.tensor.transpose(bank[0:r, (c - c0) * H:(c - c0 + 1) * H],
                                                  w0_sym[:, c * REP:c * REP + r], ident[:])
                else:
                    pe.wait_ge(small_ld, 16 * 7)
                    for c in range(B // P):
                        ins = nc.tensor.transpose(bank[0:C, c * P:(c + 1) * P], dense_in[:, c, :], ident[:])
                ins.then_inc(prep_tr, 1)

            pe.wait_ge(ident_made, 1)
            for n in range(PREP - PREP_W2):
                turn_prep(n)
            pe.wait_ge(emb_made, 1)
            turn_rows()
            pe.wait_ge(x0_made, 1)
            turn_x(0)
            for n in range(PREP - PREP_W2, PREP):
                turn_prep(n)
            layer0(0, 0, range(CHUNKS))
            pe.wait_ge(bd_made, 1)
            pe.wait_ge(emb_made, 2)
            turn_rows()
            pe.wait_ge(prep_act, PREP)
            pe.wait_ge(prep_dve, PREP_W1)
            pe.wait_ge(ones_made, 1)

            def layer1(T, h, ti, g):
                n = slice(ti * P, (ti + 1) * P)
                before, t = (g - YBANKS, T) if g >= YBANKS else (g + YBANKS, T - 1)
                if KIND[before] == "D":
                    wait(pe, dve_step, DVE_STEPS * t + DVE_DONE[before])
                else:
                    wait(pe, act_step, ACT_STEPS * t + ACT_GROUPS.index(before) + 1)
                cols = slice(FIRST[g] * H, (FIRST[g] + SIZES[g]) * H)
                y = ps_y[:, g % YBANKS, 0:SIZES[g] * H]
                hi, lo = x1_hi[:, h, n], x1_lo[:, h, n]
                nc.tensor.matmul(y, hi, w1_hi[:, cols], start=True, stop=False)
                nc.tensor.matmul(y, hi, w1_lo[:, cols], start=False, stop=False)
                nc.tensor.matmul(y, lo, w1_hi[:, cols], start=False, stop=True).then_inc(y_made, 1)

            def sum_d(T, tau):
                tau = tau % (2 * QT)
                if not isinstance(T, int) or T >= 0:
                    wait(pe, join_step, JOIN_STEPS * (T + 1))
                    wait(pe, bd_made, T // QT + 1 if isinstance(T, int) else 0)
                    wait(pe, g_kept, T)
                    nc.tensor.matmul(ps_g[:, 0:(F + 1) * TB], x2[:, tau % 2, :],
                                     bd[:, tau // QT, tau % QT].rearrange("p j b -> p (j b)"),
                                     start=True, stop=True).then_inc(g_summed, 1)

            def pair_products(i, last):
                for tau in range(2 * QT):
                    h, ti = tau // QT, tau % QT
                    q, T = 2 * i + h, 2 * QT * i + tau
                    nxt = not (last and h == 1)
                    if ti == 0:
                        wait(pe, x1_lo_made, q + 1)
                    for g in range(GROUPS):
                        if g == 7 and ti == 3 and not last:
                            wait(pe, emb_made, q + 3)
                        layer1(T, h, ti, g)
                        if g == 4:
                            wait(pe, bd_made, q + 1 if ti < 3 or not nxt else q + 2)
                            if nxt and ti == 1:
                                wait(pe, x0_made, q + 2)
                            sum_d(T - 2, tau - 2)
                            if nxt and ti == 1:
                                turn_x(1 - h)
                        if g == 7 and ti == 3 and not last:
                            turn_rows()
                        if nxt and (ti, g) in SUMMED_AFTER:
                            layer0(q + 1, 1 - h, SUMMED_AFTER[ti, g])

            pair_products(0, False)
            with pe.Fori(1, PAIRS - 1) as i:
                pair_products(i, False)
            pair_products(PAIRS - 1, True)
            sum_d(TILES - 2, TILES - 2)

            def mlp1(c, rows_c, z, start, stop):
                for m in range(MC1):
                    ins = nc.tensor.matmul(ps_y[:, m, :], wt1[0:rows_c, c, m * P:(m + 1) * P], z,
                                           start=start, stop=stop)
                    if stop:
                        ins.then_inc(h1_summed, 1)

            pe.wait_ge(late_mlp, 64)
            pe.wait_ge(r1_done, 1)
            pe.wait_ge(act_step, ACT_STEPS * TILES)
            pe.wait_ge(dve_step, DVE_STEPS * TILES)
            mlp1(0, P, r1[:], True, False)
            mlp1(3, C, dense_t, False, False)
            sum_d(TILES - 1, TILES - 1)
            pe.wait_ge(late_w2, 16)
            pe.wait_ge(g_kept, TILES)
            mlp1(1, P, g_all[:, F, :], False, False)
            for j in range(F):
                ins = nc.tensor.matmul(ps_x1[:], w2t[:, j * H:(j + 1) * H], g_all[:, j, :],
                                       start=j == 0, stop=j == F - 1)
            ins.then_inc(r3_summed, 1)
            pe.wait_ge(r3_made, 1)
            mlp1(2, P, r3, False, True)
            for m in range(MC2):
                dst = ps_y[:, YBANKS - 1, :] if m == 0 else ps_g[:]
                for c in range(MC1):
                    if m == 0:
                        pe.wait_ge(h1_made, c + 1)
                    ins = nc.tensor.matmul(dst, wt2[:, c, m * P:(m + 1) * P], h1[:, c, :],
                                           start=c == 0, stop=c == MC1 - 1)
                ins.then_inc(h2_summed, 1)
            for m in range(MC2):
                pe.wait_ge(h2_made, m + 1)
                ins = nc.tensor.matmul(ps_tr[0:1, :], wt3[:, m:m + 1], h2[:, m, :], start=m == 0, stop=m == MC2 - 1)
            ins.then_inc(y_summed, 1)


_TABLES = [f"tbl_{f}" for f in range(F)]
_REST = ["W_top1", "b_top1", "W_top2", "b_top2", "W_top3", "L0_rec_W0", "L0_rec_b0", "L0_rec_W1", "L0_rec_b1",
         "L0_rec_W2", "L0_rec_b2"]


def kernel(**inputs):
    import numpy as _np
    import concourse.bacc as _bacc
    from concourse import mybir as _mybir
    from concourse.bass_utils import run_bass_kernel_spmd as _run

    nc = _bacc.Bacc("TRN2", target_bir_lowering=False, num_devices=1)
    table = _np.concatenate([_np.asarray(inputs[t]) for t in _TABLES], axis=0)
    heights = [inputs[t].shape[0] for t in _TABLES]
    ids = _np.zeros((B, GATHERS * FPG), _np.int32)
    ids[:, :F] = _np.asarray(inputs["ids"])
    ids = ids.reshape(QUADS, QB, GATHERS, FPG).transpose(3, 1, 0, 2).reshape(P, QUADS * GATHERS)
    bases = _np.zeros((FPG, QB, GATHERS), _np.int32)
    for f in range(F):
        bases[f % FPG, :, f // FPG] = sum(heights[:f])
    laid_out = {"ids": ids, "bases": bases.reshape(P, GATHERS), "table": table, "dense_ctx": inputs["dense_ctx"]}
    laid_out.update({name: inputs[name] for name in _REST})
    arrays, aps = {}, {}
    for name, a in laid_out.items():
        a = _np.ascontiguousarray(a)
        arrays[f"in_{name}"] = a
        aps[name] = nc.dram_tensor(f"in_{name}", a.shape, _mybir.dt.from_np(a.dtype), kind="ExternalInput").ap()
    out = nc.dram_tensor("out_y", (B, 1), F32, kind="ExternalOutput").ap()
    build(nc, aps["dense_ctx"], aps["ids"], aps["bases"], aps["table"], *[aps[n] for n in _REST], out)
    r = _run(nc, [arrays], core_ids=[0])
    return r.results[0]["out_y"]
```
